# Optimizing a Trainium2 kernel written in Bass

```python
import numpy as np
import jax
import jax.numpy as jnp

def _softmax(x, axis=-1):
    return jax.nn.softmax(x, axis=axis)

def _gelu(x):
    return jax.nn.gelu(x, approximate=True)

def _silu(x):
    return jax.nn.silu(x)

def _sigmoid(x):
    return jax.nn.sigmoid(x)

def _layernorm(x, axis=-1, eps=1e-05):
    m = jnp.mean(x, axis=axis, keepdims=True)
    v = jnp.var(x, axis=axis, keepdims=True)
    return (x - m) / jnp.sqrt(v + eps)

def _scatter_add(tgt, idx, src, axis=0):
    return tgt.at[idx].add(src)

def _segment_sum(src, seg, n):
    return jax.ops.segment_sum(src, seg, n)
kernel_name = 'mk_decoder_preln_d1_seqx_r8_e352e4'

def setup_inputs(seed: int=0):
    np.random.seed(seed)
    _w = jnp.asarray

    def _rec_inputs():
        import jax
        import jax.numpy as jnp
        _rk = jax.random.key(seed)
        x = 7.22e-05 + 1 * jax.random.normal(jax.random.fold_in(_rk, 1), (64, 64, 128), jnp.float32)
        _lenS = 64 - jax.random.randint(jax.random.fold_in(_rk, 7), (64,), 0, max(1, 64 // 4) + 1, jnp.int32)
        _lenS2 = 64 - jax.random.randint(jax.random.fold_in(_rk, 8), (64,), 0, max(1, 64 // 4) + 1, jnp.int32)
        _ctx_1024P = jax.random.normal(jax.random.fold_in(_rk, 11), (64, 16, 128), jnp.float32)
        _ctx_1024c = jax.random.dirichlet(jax.random.fold_in(_rk, 511), 0.3 * jnp.ones((16,), jnp.float32), (64, 64))
        _ctx_1024t = jnp.einsum('bsk,bkd->bsd', _ctx_1024c, _ctx_1024P)
        _ctx_1024t = _ctx_1024t * jax.lax.rsqrt(jnp.mean(jnp.square(_ctx_1024t)) + 1e-12) * 0.953939
        ctx_1024 = 4.13588e-05 + 0.999923 * (_ctx_1024t + 0.3 * jax.random.normal(jax.random.fold_in(_rk, 611), (64, 64, 128), jnp.float32))
        return (x, ctx_1024)
    x, ctx_1024 = _rec_inputs()

    def _L0_attn_setup():
        import jax, jax.numpy as jnp
        import numpy as np
        B, S, E, H, P = (2, 256, 128, 16, 256)
        HD = E // H
        key = jax.random.key(seed)
        ks = jax.random.split(key, 10)
        std = E ** (-0.5)
        x = jax.random.normal(ks[0], (B, S, E), jnp.float32)
        Wq = jax.random.normal(ks[1], (E, E), jnp.float32) * std
        Wk = jax.random.normal(ks[2], (E, E), jnp.float32) * std
        Wv = jax.random.normal(ks[3], (E, E), jnp.float32) * std
        Wo = jax.random.normal(ks[4], (E, E), jnp.float32) * std
        rel_key = jax.random.normal(ks[5], (P, HD), jnp.float32) * 0.02
        z = jnp.zeros((E,), jnp.float32)
        return {'x': x, 'Wq': Wq, 'bq': z, 'Wk': Wk, 'bk': z, 'Wv': Wv, 'bv': z, 'Wo': Wo, 'bo': z, 'rel_key': rel_key}
    _L0_attn_all = _L0_attn_setup()
    _L0_attn_in = {k: v for k, v in _L0_attn_all.items() if k in ('Wq', 'bq', 'Wk', 'bk', 'Wv', 'bv', 'Wo', 'bo', 'rel_key')}
    del _L0_attn_all

    def _L0_xattn_setup():
        import jax, jax.numpy as jnp
        import numpy as np
        D_MODEL = 128
        N_HEADS = 16
        HEAD_DIM = D_MODEL // N_HEADS
        key = jax.random.key(seed)
        ks = jax.random.split(key, 12)
        B, L = (4, 256)
        s = 1.0 / np.sqrt(D_MODEL)
        inp = {'q': jax.random.normal(ks[0], (B, L, D_MODEL), jnp.float32), 'k': jax.random.normal(ks[1], (B, L, D_MODEL), jnp.float32), 'v': jax.random.normal(ks[2], (B, L, D_MODEL), jnp.float32), 'Wq': jax.random.normal(ks[3], (D_MODEL, D_MODEL), jnp.float32) * s, 'bq': jax.random.normal(ks[4], (D_MODEL,), jnp.float32) * 0.01, 'Wk': jax.random.normal(ks[5], (D_MODEL, D_MODEL), jnp.float32) * s, 'bk': jax.random.normal(ks[6], (D_MODEL,), jnp.float32) * 0.01, 'Wv': jax.random.normal(ks[7], (D_MODEL, D_MODEL), jnp.float32) * s, 'bv': jax.random.normal(ks[8], (D_MODEL,), jnp.float32) * 0.01, 'Wo': jax.random.normal(ks[9], (D_MODEL, D_MODEL), jnp.float32) * s, 'bo': jax.random.normal(ks[10], (D_MODEL,), jnp.float32) * 0.01}
        return inp
    _L0_xattn_all = _L0_xattn_setup()
    _L0_xattn_in = {k: v for k, v in _L0_xattn_all.items() if k in ('Wq', 'bq', 'Wk', 'bk', 'Wv', 'bv', 'Wo', 'bo')}
    del _L0_xattn_all

    def _L0_ffn_setup():
        import jax, jax.numpy as jnp
        import numpy as np
        E = 8
        K = 2
        R = 64
        ALPHA = 128.0
        SCALING = ALPHA / R
        key = jax.random.key(seed)
        k0, k1, k2, k3 = jax.random.split(key, 4)
        B, S, D = (4, 512, 128)
        x = jax.random.normal(k0, (B, S, D), jnp.float32)
        Wg = jax.random.normal(k1, (E, D), jnp.float32) * 0.02
        bg = jnp.zeros((E,), jnp.float32)
        W1 = jax.random.normal(k2, (E, R, D), jnp.float32) * (1.0 / np.sqrt(D))
        W2 = jax.random.normal(k3, (E, D, R), jnp.float32) * 0.02
        return {'x': x, 'Wg': Wg, 'bg': bg, 'W1': W1, 'W2': W2}
    _L0_ffn_all = _L0_ffn_setup()
    _L0_ffn_in = {k: v for k, v in _L0_ffn_all.items() if k in ('Wg', 'bg', 'W1', 'W2')}
    del _L0_ffn_all
    return {'x': x, 'ctx_1024': ctx_1024, 'L0_attn_Wq': _L0_attn_in['Wq'], 'L0_attn_bq': _L0_attn_in['bq'], 'L0_attn_Wk': _L0_attn_in['Wk'], 'L0_attn_bk': _L0_attn_in['bk'], 'L0_attn_Wv': _L0_attn_in['Wv'], 'L0_attn_bv': _L0_attn_in['bv'], 'L0_attn_Wo': _L0_attn_in['Wo'], 'L0_attn_bo': _L0_attn_in['bo'], 'L0_attn_rel_key': _L0_attn_in['rel_key'], 'L0_xattn_Wq': _L0_xattn_in['Wq'], 'L0_xattn_bq': _L0_xattn_in['bq'], 'L0_xattn_Wk': _L0_xattn_in['Wk'], 'L0_xattn_bk': _L0_xattn_in['bk'], 'L0_xattn_Wv': _L0_xattn_in['Wv'], 'L0_xattn_bv': _L0_xattn_in['bv'], 'L0_xattn_Wo': _L0_xattn_in['Wo'], 'L0_xattn_bo': _L0_xattn_in['bo'], 'L0_ffn_Wg': _L0_ffn_in['Wg'], 'L0_ffn_bg': _L0_ffn_in['bg'], 'L0_ffn_W1': _L0_ffn_in['W1'], 'L0_ffn_W2': _L0_ffn_in['W2']}

def reference(x, ctx_1024, L0_attn_Wq, L0_attn_bq, L0_attn_Wk, L0_attn_bk, L0_attn_Wv, L0_attn_bv, L0_attn_Wo, L0_attn_bo, L0_attn_rel_key, L0_xattn_Wq, L0_xattn_bq, L0_xattn_Wk, L0_xattn_bk, L0_xattn_Wv, L0_xattn_bv, L0_xattn_Wo, L0_xattn_bo, L0_ffn_Wg, L0_ffn_bg, L0_ffn_W1, L0_ffn_W2):
    import jax
    import jax.numpy as jnp

    def _L0_attn_ref(x, Wq, bq, Wk, bk, Wv, bv, Wo, bo, rel_key):
        import jax, jax.numpy as jnp
        import numpy as np
        B, S, E, H, P = (2, 256, 128, 16, 256)
        HD = E // H
        b, s, e = x.shape
        p, hd = rel_key.shape
        h = e // hd
        scale = hd ** (-0.5)

        def split_heads(t):
            return t.reshape(b, s, h, hd).transpose(0, 2, 1, 3)
        q = split_heads(x @ Wq + bq)
        k = split_heads(x @ Wk + bk)
        v = split_heads(x @ Wv + bv)
        scores = jnp.einsum('bhid,bhjd->bhij', q, k)
        rel = jnp.einsum('bhid,pd->bhip', q, rel_key)
        i = jnp.arange(s)[:, None]
        j = jnp.arange(s)[None, :]
        rel_idx = jnp.clip(j - i + p - 1, 0, p - 1)
        bias = jnp.take_along_axis(rel, jnp.broadcast_to(rel_idx[None, None], (b, h, s, s)), axis=3)
        causal = j <= i
        logits = jnp.where(causal[None, None], (scores + bias) * scale, -jnp.inf)
        attn = jax.nn.softmax(logits, axis=-1)
        out = jnp.einsum('bhij,bhjd->bhid', attn, v)
        out = out.transpose(0, 2, 1, 3).reshape(b, s, e)
        return out @ Wo + bo

    def _L0_xattn_ref(q, k, v, Wq, bq, Wk, bk, Wv, bv, Wo, bo):
        import jax, jax.numpy as jnp
        import numpy as np
        D_MODEL = 128
        N_HEADS = 16
        HEAD_DIM = D_MODEL // N_HEADS
        B, L, _ = q.shape
        Q = q @ Wq.T + bq
        K = k @ Wk.T + bk
        V = v @ Wv.T + bv
        Q = Q.reshape(B, L, N_HEADS, HEAD_DIM).transpose(0, 2, 1, 3)
        K = K.reshape(B, L, N_HEADS, HEAD_DIM).transpose(0, 2, 1, 3)
        V = V.reshape(B, L, N_HEADS, HEAD_DIM).transpose(0, 2, 1, 3)
        energy = jnp.einsum('bhqd,bhkd->bhqk', Q, K)
        attn = jax.nn.softmax(energy, axis=-1)
        x = jnp.einsum('bhqk,bhkd->bhqd', attn, V)
        x = x.transpose(0, 2, 1, 3).reshape(B, L, D_MODEL)
        return x @ Wo.T + bo

    def _L0_ffn_ref(x, Wg, bg, W1, W2):
        import jax, jax.numpy as jnp
        import numpy as np
        E = 8
        K = 2
        R = 64
        ALPHA = 128.0
        SCALING = ALPHA / R
        orig_shape = x.shape
        D = orig_shape[-1]
        xf = x.reshape(-1, D)
        logits = xf @ Wg.T + bg
        top_gates, top_idx = jax.lax.top_k(logits, K)
        top_gates = jax.nn.softmax(top_gates, axis=-1)
        h = jax.nn.gelu(jnp.einsum('nd,erd->enr', xf, W1), approximate=False)
        eout = SCALING * jnp.einsum('enr,edr->ned', h, W2)
        sel = jnp.take_along_axis(eout, top_idx[:, :, None], axis=1)
        out = jnp.sum(top_gates[:, :, None] * sel, axis=1)
        return out.reshape(orig_shape)
    x = x + _L0_attn_ref(_layernorm(x, axis=-1), L0_attn_Wq, L0_attn_bq, L0_attn_Wk, L0_attn_bk, L0_attn_Wv, L0_attn_bv, L0_attn_Wo, L0_attn_bo, L0_attn_rel_key)
    x = x + _L0_xattn_ref(_layernorm(x, axis=-1), ctx_1024, ctx_1024, L0_xattn_Wq, L0_xattn_bq, L0_xattn_Wk, L0_xattn_bk, L0_xattn_Wv, L0_xattn_bv, L0_xattn_Wo, L0_xattn_bo)
    x = x + _L0_ffn_ref(_layernorm(x, axis=-1), L0_ffn_Wg, L0_ffn_bg, L0_ffn_W1, L0_ffn_W2)
    return x

_drawn_inputs = setup_inputs


def setup_inputs(seed=0):
    import zlib

    import numpy as np

    out = dict(_drawn_inputs(seed))
    spreads = {'L0_attn_bq': (0.0, 0.273),
     'L0_attn_bk': (0.0, 0.8),
     'L0_attn_bv': (0.0, 0.1),
     'L0_attn_bo': (0.0, 0.1),
     'L0_ffn_bg': (0.0, 0.1)}
    factors = {'L0_attn_rel_key': 7.204,
     'L0_xattn_bq': 6.332,
     'L0_xattn_bk': 8.0,
     'L0_xattn_bv': 4.937,
     'L0_xattn_bo': 4.422}
    for name, (base, spread) in spreads.items():
        noise = np.random.default_rng([zlib.crc32(name.encode()), seed]).standard_normal(out[name].shape)
        drawn = base * np.exp(spread * noise) if base else spread * noise
        out[name] = jnp.asarray(drawn.astype(out[name].dtype))
    for name, factor in factors.items():
        out[name] = (out[name] * factor).astype(out[name].dtype)
    return out
```

```python
import concourse.bass as bass
import concourse.mybir as mybir
from concourse.alu_op_type import AluOpType as ALU

F32 = mybir.dt.float32
BF16 = mybir.dt.bfloat16
U32 = mybir.dt.uint32
ACT = mybir.ActivationFunctionType
AX = mybir.AxisListType

B, S, D = 64, 64, 128
H, HD = 16, 8
HP = H // 2
NPAIR = B // 2
CP = 4
NCH = NPAIR // CP
CT = CP * 128
HALF = CT // 2
SC = H * S
E, R = 8, 64
NC4 = E * R // 128
TOPK = 2
LORA = 2.0
EPS = 1e-5
NEG = -1.0e30
NSPLIT = 3
QPART = (0, 0, 1, 0, 1, 2)
KPART = (0, 1, 0, 2, 1, 0)
NPROD = len(QPART)
KROWS = 64 + NPROD * HD
VW = 18


def build(nc, x_in, ctx_in, w, out):
    from contextlib import ExitStack
    ctx = ExitStack()
    with ctx:
        def sb(name, shape, dt=F32):
            return ctx.enter_context(nc.sbuf_tensor(name, shape, dt))

        def sem(name):
            return ctx.enter_context(nc.semaphore(name))

        X = sb("X", [128, NPAIR, D])
        ident = sb("ident", [128, 128])
        identb = sb("identb", [128, 128], BF16)
        maskneg = sb("maskneg", [128, S], BF16)
        ones = sb("ones", [1, 128])
        wt = {}
        for a in (1, 2):
            for n in "qkvo":
                wt[n, a] = sb(f"w{n}{a}", [128, D])
        brow = sb("brow", [1, 4, D])
        bcol = sb("bcol", [128, 4])
        relw = sb("relw", [128, H, S])
        wg = sb("wg", [128, E])
        bg = sb("bg", [1, CP, E])
        w1 = sb("w1", [128, E * R])
        w2 = sb("w2", [128, NC4, D])
        sel = sb("sel", [E, E * R])
        iota8 = sb("iota8", [128, E])
        nhalf = sb("nhalf", [128, CP])
        ecst = sb("ecst", [128, CP])
        Qst = sb("Qst", [128, 2, H, 2, HALF], BF16)
        Kst = sb("Kst", [128, 2, H, HALF], BF16)
        V = sb("V", [128, NPAIR * 2, HP, VW])
        st6 = sb("st6", [128, CP, 6])
        mv = sb("mv", [128, CP, 2])
        veps = sb("veps", [128, CP])
        rstd = sb("rstd", [128, CP])
        xn = sb("xn", [128, CP, D])
        xnT = sb("xnT", [128, 2, CT])
        cx = sb("cx", [128, 2, CP, D])
        cxT = sb("cxT", [128, 2, CT])
        qk = sb("qk", [128, 2, CT])
        qkr = sb("qkr", [128, 2, CT])
        parts = sb("parts", [128, 2, 2, NSPLIT, CT], BF16)
        relst = sb("relst", [128, 2, SC])
        relsh = sb("relsh", [128, 4, SC])
        SS = sb("SS", [128, 2, H, S])
        negm = sb("negm", [128, 2, H])
        nhi = sb("nhi", [128, 2, H], BF16)
        nlo = sb("nlo", [128, 2, H], BF16)
        P = sb("P", [128, 2, SC])
        PT = sb("PT", [128, 2, SC])
        idle = sb("idle", [128, 1])
        rden = sb("rden", [128, H])
        on = sb("on", [128, 2, CP, D])
        onT = sb("onT", [128, CT])
        lg = sb("lg", [128, CP, E])
        mx = sb("mx", [128, CP, 8])
        ix = sb("ix", [128, CP, 8], U32)
        ixf = sb("ixf", [128, CP, TOPK])
        dgate = sb("dgate", [128, CP])
        egate = sb("egate", [128, CP])
        gate = sb("gate", [128, TOPK, CP])
        eq = sb("eq", [128, TOPK, CP, E])
        coef = sb("coef", [128, CP, E])
        coefT = relst[0:E, 0, 0:CT]
        hg = relsh[:, 0, :].rearrange("p (s c) -> p s c", s=2)
        hw = relsh[:, 1, :].rearrange("p (s c) -> p s c", s=2)
        yst = relsh[:, 2, :].rearrange("p (s q d) -> p s q d", s=2, d=D)

        partD = nc.dram_tensor("parts_scratch", [2, NCH, 2, 128, NSPLIT, CT], BF16, kind="Internal")
        relD = nc.dram_tensor("rel_scratch", [NPAIR, 128, SC], F32, kind="Internal")

        ps = ctx.enter_context(nc.psum_tensor("ps", [128, 8, 512], F32))

        s_w = sem("s_w")
        s_ms = sem("s_ms")
        s_cst = sem("s_cst")
        s_ctx = [sem(f"s_ctx{h}") for h in range(2)]
        s_stat = sem("s_stat")
        s_rstd = sem("s_rstd")
        s_xn = sem("s_xn")
        s_xtp = sem("s_xtp")
        s_xnT = sem("s_xnT")
        s_ctp = sem("s_ctp")
        s_cxT = sem("s_cxT")
        s_qkp = sem("s_qkp")
        s_qf = sem("s_qf")
        s_kf = sem("s_kf")
        s_r = sem("s_r")
        s_p2 = sem("s_p2")
        s_p3 = sem("s_p3")
        s_pw = [sem(f"s_pw{h}") for h in range(2)]
        s_vp = sem("s_vp")
        s_v0 = sem("s_v0")
        s_v1 = sem("s_v1")
        s_relp = sem("s_relp")
        s_re0 = sem("s_re0")
        s_re1 = sem("s_re1")
        s_rw = [sem(f"s_rw{h}") for h in range(2)]
        s_st = [sem(f"s_st{h}") for h in range(2)]
        s_rl = [sem(f"s_rl{h}") for h in range(4)]
        s_qk = sem("s_qk")
        s_add = sem("s_add")
        s_mx = sem("s_mx")
        s_sub = sem("s_sub")
        s_p = sem("s_p")
        s_t = sem("s_t")
        s_e0 = sem("s_e0")
        s_e1 = sem("s_e1")
        s_pv = sem("s_pv")
        s_on = sem("s_on")
        s_ot = sem("s_ot")
        s_onT = sem("s_onT")
        s_wo = sem("s_wo")
        s_x = sem("s_x")
        c_dve = [sem(f"c_dve{n}") for n in range(5)]
        s_lgp = sem("s_lgp")
        s_dg = sem("s_dg")
        s_eg = sem("s_eg")
        s_cf = sem("s_cf")
        s_cfp = sem("s_cfp")
        s_cfT = sem("s_cfT")
        s_h = sem("s_h")
        s_hb = sem("s_hb")
        s_g = sem("s_g")
        s_hw = sem("s_hw")
        s_y = sem("s_y")
        s_yo = sem("s_yo")
        s_out = [sem(f"s_out{h}") for h in range(2)]

        NWDMA = 1 + 8 + 4 + 4 + 1 + CP + 2 + H

        def wait(eng, s, n):
            if isinstance(n, int) and n <= 0:
                return
            eng.wait_ge(s, n)

        def chunks(eng, body, first=0):
            for h in range(2):
                body(h, h, 0)
            with eng.Fori(1, NCH // 2) as i:
                for h in range(2):
                    body(i * 2 + h, h, i)

        def steps(eng, body, last):
            for u in range(8):
                body(u, u, 0)
            with eng.Fori(1, NPAIR // 8) as i:
                for u in range(8):
                    body(i * 8 + u, u, i)
            for u in range(last):
                body(NPAIR + u, u, None)

        def live(t, u, i, lag):
            if i is None:
                return u - lag < 0
            return not isinstance(t, int) or t >= lag

        def slot2(u):
            return u % 2

        block = ctx.enter_context(nc.Block())

        @block.sync
        def _(sp):
            xv = x_in.rearrange("(q b) s d -> (b s) q d", b=2)
            sp.dma_start(X[:, :, :], xv).then_inc(s_w, 16)
            for a in (1, 2):
                for n in "qkvo":
                    sp.dma_start(wt[n, a][:, :], w[f"W{n}{a}"]).then_inc(s_w, 16)
            for k, n in enumerate(("bv1", "bo1", "bv2", "bo2")):
                sp.dma_start(brow[0:1, k, :], w[n]).then_inc(s_w, 16)
            for k, n in enumerate(("bq1", "bk1", "bq2", "bk2")):
                sp.dma_start(bcol[:, k:k + 1], w[n]).then_inc(s_w, 16)
            sp.dma_start(wg[:, :], w["Wg"]).then_inc(s_w, 16)
            for k in range(CP):
                sp.dma_start(bg[0:1, k, :], w["bg"]).then_inc(s_w, 16)
            sp.dma_start(w1[:, :], w["W1"]).then_inc(s_w, 16)
            sp.dma_start(w2[:, :, :], w["W2"].rearrange("(c p) d -> p c d", p=128)).then_inc(s_w, 16)
            sp.wait_ge(s_ms, 1)
            for h in range(H):
                sp.dma_start(relw[h * HD:(h + 1) * HD, h, :], w["rel"]).then_inc(s_w, 16)
            sp.wait_ge(s_ms, 3)

            ctxv = ctx_in.rearrange("(q b) s d -> (b s) q d", b=2)
            for a in (1, 2):
                n0 = (a - 1) * NCH

                def project(c, h, i):
                    if a == 2:
                        wait(sp, s_ctp, c - 1)
                        sp.dma_start(cx[:, h, :, :], ctxv[:, bass.ds(c * CP, CP), :]).then_inc(s_ctx[h], 16)
                    wait(sp, s_p3, 2 * (c + 1 + n0))
                    for z in range(2):
                        sp.dma_start(
                            bass.AP(partD, ((((a - 1) * NCH + c) * 2 + z) * 128) * NSPLIT * CT,
                                    [[NSPLIT * CT, 128], [1, NSPLIT * CT]]),
                            parts[:, h, z, :, :].rearrange("p s c -> p (s c)")).then_inc(s_pw[h], 16)
                    if a == 1:
                        for k in range(CP):
                            t = c * CP + k
                            wait(sp, s_re0, t + 1)
                            wait(sp, s_re1, t + 1)
                            sp.dma_start(bass.AP(relD, t * 128 * SC, [[SC, 128], [1, SC]]),
                                         relst[:, k % 2, :]).then_inc(s_rw[k % 2], 16)
                chunks(sp, project)

                def load_stack(c, h):
                    wait(sp, s_qk, (c - 1) * CP + (a - 1) * NPAIR)
                    base = ((a - 1) * NCH + c) * 2 * 128 * NSPLIT * CT
                    for par in range(2):
                        for m in range(NPROD):
                            r0 = 64 * par + m * HD
                            for z, part in ((0, QPART[m]), (1, KPART[m])):
                                src = bass.AP(partD, base + z * 128 * NSPLIT * CT + part * CT + par * HALF,
                                              [[NSPLIT * CT, HD], [HD * NSPLIT * CT, H], [1, HALF]])
                                dst = Qst[r0:r0 + HD, h, :, par, :] if z == 0 else Kst[r0:r0 + HD, h, :, :]
                                sp.dma_start(dst, src).then_inc(s_st[h], 16)

                def load_rel(t, k):
                    if isinstance(t, int) and t < 4:
                        pass
                    else:
                        sp.wait_ge(s_add, t - 3)
                    for par in range(2):
                        src = bass.AP(relD, t * 128 * SC + par * 64 * SC + (S - 1), [[SC - 1, 64], [1, SC]])
                        sp.dma_start(relsh[par * 64:par * 64 + 64, k, :], src).then_inc(s_rl[k], 16)

                for h in range(2):
                    sp.wait_ge(s_pw[h], 32 * (NCH // 2) * a)
                if a == 1:
                    for h in range(2):
                        sp.wait_ge(s_rw[h], 16 * (NPAIR // 2))

                def attend(c, h, i):
                    load_stack(c, h)
                    if a == 1:
                        for k in range(CP):
                            load_rel(c * CP + k, k)
                chunks(sp, attend)

            def store(c, h, i):
                wait(sp, s_y, c + 1)
                outv = out.rearrange("(q b) s d -> (b s) q d", b=2)
                sp.dma_start(outv[:, bass.ds(c * CP, CP), :], yst[:, h, :, :]).then_inc(s_out[h], 16)
            chunks(sp, store)
            for h in range(2):
                sp.wait_ge(s_out[h], 16 * (NCH // 2))

        @block.gpsimd
        def _(pool):
            g = nc.gpsimd
            g.memset(relw[:, :, :], 0.0).then_inc(s_ms, 1)
            g.memset(Qst[:, :, :, :, :], 0.0).then_inc(s_ms, 1)
            g.memset(Kst[:, :, :, :], 0.0).then_inc(s_ms, 1)
            g.memset(V[:, :, :, :], 0.0).then_inc(s_ms, 1)
            g.memset(ident[:, :], 0.0).then_inc(s_ms, 1)
            g.memset(maskneg[:, :], 0.0).then_inc(s_ms, 1)
            g.memset(sel[:, :], 1.0).then_inc(s_ms, 1)
            g.memset(ones[:, :], 1.0).then_inc(s_ms, 1)
            g.memset(nhalf[:, :], -0.5).then_inc(s_ms, 1)
            g.memset(ecst[:, :], 2.718281828459045).then_inc(s_ms, 1)
            g.iota(iota8[:, :], pattern=[[1, E]], base=0, channel_multiplier=0,
                   allow_small_or_imprecise_dtypes=True).then_inc(s_ms, 1)
            pool.wait_ge(s_ms, 11)
            g.memset(V[0:64, :, :, 2 * HD:2 * HD + 1], 1.0).then_inc(s_cst, 1)
            pool.wait_ge(s_cst, 1)
            g.memset(V[64:128, :, :, 2 * HD + 1:VW], 1.0).then_inc(s_cst, 1)
            pool.wait_ge(s_cst, 2)
            g.affine_select(out=ident[:, :], in_=ident[:, :], compare_op=ALU.not_equal, fill=1.0,
                            base=0, pattern=[[-1, 128]], channel_multiplier=1).then_inc(s_cst, 1)
            for par in range(2):
                pool.wait_ge(s_cst, 3 + par)
                v = maskneg[par * 64:par * 64 + 64, :]
                g.affine_select(out=v, in_=v, compare_op=ALU.is_ge, fill=NEG, base=0,
                                pattern=[[-1, S]], channel_multiplier=1).then_inc(s_cst, 1)
            pool.wait_ge(s_cst, 5)
            g.affine_select(out=sel[:, :], in_=sel[:, :], compare_op=ALU.is_ge, fill=0.0, base=0,
                            pattern=[[1, E * R]], channel_multiplier=-R).then_inc(s_cst, 1)
            pool.wait_ge(s_cst, 6)
            g.affine_select(out=sel[:, :], in_=sel[:, :], compare_op=ALU.is_ge, fill=0.0, base=R - 1,
                            pattern=[[-1, E * R]], channel_multiplier=R).then_inc(s_cst, 1)
            g.tensor_copy(identb[:, :], ident[:, :]).then_inc(s_cst, 1)

            def power(n):
                wait(pool, s_stat, n + 1)
                g.tensor_tensor(rstd[:, :], veps[:, :], nhalf[:, :], ALU.pow).then_inc(s_rstd, 1)

            for a in (1, 2):
                n0 = (a - 1) * NCH

                def project(c, h, i):
                    power(c + n0)
                    wait(pool, s_qf, 2 * (c + n0 + 1))
                    g.tensor_tensor(qkr[:, 0, :], qk[:, 0, :], parts[:, h, 0, 0, :], ALU.subtract).then_inc(s_r, 1)
                    wait(pool, s_p2, c + n0 + 1)
                    g.tensor_tensor(parts[:, h, 0, 2, :], qkr[:, 0, :], parts[:, h, 0, 1, :],
                                    ALU.subtract).then_inc(s_p3, 1)
                chunks(pool, project)
                if a == 1:
                    def attend(t, u, i):
                        wait(pool, s_mx, t + 1)
                        v = SS[:, slot2(u), :, :]
                        g.tensor_tensor(v, v, negm[:, slot2(u), :].unsqueeze(2).broadcast_to([128, H, S]),
                                        ALU.add).then_inc(s_sub, 1)
                    steps(pool, attend, 0)

            def ffn(c, h, i):
                power(c + 2 * NCH)
                wait(pool, s_dg, c + 1)
                g.tensor_tensor(egate[:, :], ecst[:, :], dgate[:, :], ALU.pow).then_inc(s_eg, 1)
            chunks(pool, ffn)

        @block.scalar
        def _(act):
            A = nc.scalar
            act.wait_ge(s_w, 16 * NWDMA)
            act.wait_ge(s_ms, 11)
            for a in (1, 2):
                n0 = (a - 1) * NCH
                t0 = (a - 1) * NPAIR

                def project(c, h, i):
                    wait(act, s_xtp, c + n0 + 1)
                    wait(act, s_vp, c + n0 - 1)
                    A.copy(xnT[:, h, :], ps[:, 0, :]).then_inc(s_xnT, 1)
                    if a == 2:
                        wait(act, s_ctp, c + 1)
                        A.copy(cxT[:, h, :], ps[:, 1, :]).then_inc(s_cxT, 1)
                    wait(act, s_qkp, c + n0 + 1)
                    qv = ps[:, 2, :].rearrange("p (q b i) -> p b i q", b=2, i=S)
                    bq = bcol[:, 2 * a - 2:2 * a - 1]
                    wait(act, s_r, c + n0)
                    if a == 1:
                        wait(act, s_relp, c * CP)
                    A.activation(qk[:, 0, :].rearrange("p (b i q) -> p b i q", b=2, i=S), qv,
                                 ACT.Identity, bias=bq).then_inc(s_qf, 1)
                    if a == 2 or not isinstance(c, int) or c >= 2:
                        if a == 1:
                            act.wait_ge(s_pw[h], 32 * i)
                        else:
                            act.wait_ge(s_pw[h], 32 * (i + NCH // 2))
                    A.activation(parts[:, h, 0, 0, :].rearrange("p (b i q) -> p b i q", b=2, i=S), qv,
                                 ACT.Identity, bias=bq).then_inc(s_qf, 1)
                    wait(act, s_vp, c + n0 + 1)
                    if a == 2:
                        act.wait_ge(s_pv, NPAIR)
                    A.copy(V[0:64, bass.ds(c * 2 * CP, 2 * CP), :, 0:HD],
                           ps[0:64, 4, :].rearrange("p (b g d) -> p b g d", g=HP, d=HD)).then_inc(s_v0, 1)
                    wait(act, s_r, c + n0 + 1)
                    A.copy(parts[:, h, 0, 1, :], qkr[:, 0, :]).then_inc(s_p2, 1)
                    if a == 1:
                        for k in range(CP):
                            t = c * CP + k
                            wait(act, s_relp, t + 1)
                            if k >= 2 or not isinstance(c, int) or c >= 1:
                                act.wait_ge(s_rw[k % 2], (c * 2 + k // 2) * 16)
                            A.copy(relst[:, k % 2, 0:512], ps[:, 6, :]).then_inc(s_re0, 1)
                chunks(act, project)

                def attend(t, u, i):
                    if live(t, u, i, 1):
                        v = (u - 1) % 2
                        wait(act, s_t, 2 * (t + t0 - 2))
                        if a == 1:
                            wait(act, s_sub, t)
                            A.activation(P[:, v, :], SS[:, v, :, :].rearrange("p h j -> p (h j)"), ACT.Exp,
                                         scale=HD ** -0.5).then_inc(s_p, 1)
                        else:
                            wait(act, s_sub, t + t0)
                            A.activation(P[:, v, :], ps[:, 2 * v:2 * v + 2, :].rearrange("p k c -> p (k c)"),
                                         ACT.Exp).then_inc(s_p, 1)
                    if live(t, u, i, 2):
                        wait(act, s_t, 2 * (t + t0 - 2) + 1)
                        wait(act, s_pv, t + t0 - 3)
                        A.copy(PT[:, u % 2, 0:512], ps[:, 4, :]).then_inc(s_e0, 1)
                    if u % 4 == 3 and live(t, u, i, 4):
                        c = (t + t0 - 3)
                        if isinstance(t, int):
                            cn = (t + t0 - 3) // 4
                        else:
                            cn = i * 2 + (u - 3) // 4 + (a - 1) * NCH
                        wait(act, s_ot, cn)
                        A.copy(onT[:, :], ps[:, 7, :]).then_inc(s_onT, 1)
                steps(act, attend, 4)

            def ffn(c, h, i):
                wait(act, s_xtp, c + 2 * NCH + 1)
                wait(act, s_h, 4 * (c - 1))
                A.copy(xnT[:, h, :], ps[:, 0, :]).then_inc(s_xnT, 1)
                wait(act, s_cfp, c + 1)
                wait(act, s_hb, 4 * c)
                A.copy(coefT[:, :], ps[0:E, 2, :]).then_inc(s_cfT, 1)
                for k in range(NC4):
                    wait(act, s_h, 4 * c + k + 1)
                    wait(act, s_hw, 4 * c + k - 1)
                    A.activation(hg[:, k % 2, :], ps[:, 4 + k % 2, :], ACT.Gelu).then_inc(s_g, 1)
            chunks(act, ffn)

        @block.vector
        def _(dve):
            v = nc.vector
            dve.wait_ge(s_w, 16 * NWDMA)
            dve.wait_ge(s_ms, 11)

            class Chain:
                def __init__(self, s, per):
                    self.s, self.per, self.n, self.base = s, per, 0, 0

                def at(self, i):
                    self.base, self.n = (i * self.per if i is not None else self.base), 0 if i is not None else self.n

                def link(self, ins):
                    ins.then_inc(self.s, 1)
                    self.n += 1
                    dve.wait_ge(self.s, self.base + self.n)

            def norm(n, c, ch):
                wait(dve, s_rstd, n)
                for k in range(CP):
                    last = v.bn_stats(st6[:, k, :], X[:, c * CP + k, :])
                ch.link(last)
                v.memset(idle[:, :], 0.0)
                for k in range(CP):
                    last = v.bn_aggr(mv[:, k, :], st6[:, k, :])
                ch.link(last)
                v.tensor_scalar(veps[:, :], mv[:, :, 1], EPS, None, ALU.add).then_inc(s_stat, 1)
                wait(dve, s_rstd, n + 1)
                wait(dve, s_xtp, n)
                for k in range(CP):
                    last = v.tensor_scalar(xn[:, k, :], X[:, c * CP + k, :], mv[:, k, 0:1], rstd[:, k:k + 1],
                                           ALU.subtract, ALU.mult)
                last.then_inc(s_xn, 1)

            for a in (1, 2):
                n0 = (a - 1) * NCH
                t0 = (a - 1) * NPAIR
                if a == 2:
                    dve.wait_ge(s_x, NCH)
                chp = Chain(c_dve[a - 1], 2 * 2)

                def project(c, h, i):
                    if h == 0:
                        chp.at(i)
                    norm(c + n0, c, chp)
                    wait(dve, s_qkp, c + n0 + 1)
                    kv = ps[:, 3, :].rearrange("p (q b i) -> p b q i", b=2, i=S)
                    bk = bcol[:, 2 * a - 1:2 * a]
                    v.tensor_scalar(qk[:, 1, :].rearrange("p (b q i) -> p b q i", b=2, i=S), kv, bk, None,
                                    ALU.add).then_inc(s_kf, 1)
                    if a == 2 or not isinstance(c, int) or c >= 2:
                        if a == 1:
                            dve.wait_ge(s_pw[h], 32 * i)
                        else:
                            dve.wait_ge(s_pw[h], 32 * (i + NCH // 2))
                    v.tensor_scalar(parts[:, h, 1, 0, :].rearrange("p (b q i) -> p b q i", b=2, i=S), kv, bk, None,
                                    ALU.add).then_inc(s_kf, 1)
                    dve.wait_ge(s_kf, 4 * (c + n0 + 1) - 2)
                    v.tensor_tensor(qkr[:, 1, :], qk[:, 1, :], parts[:, h, 1, 0, :], ALU.subtract).then_inc(s_kf, 1)
                    dve.wait_ge(s_kf, 4 * (c + n0 + 1) - 1)
                    v.tensor_copy(parts[:, h, 1, 1, :], qkr[:, 1, :]).then_inc(s_kf, 1)
                    dve.wait_ge(s_kf, 4 * (c + n0 + 1))
                    v.tensor_tensor(parts[:, h, 1, 2, :], qkr[:, 1, :], parts[:, h, 1, 1, :],
                                    ALU.subtract).then_inc(s_p3, 1)
                    wait(dve, s_vp, c + n0 + 1)
                    if a == 2:
                        dve.wait_ge(s_pv, NPAIR)
                    v.tensor_copy(V[64:128, bass.ds(c * 2 * CP, 2 * CP), :, HD:2 * HD],
                                  ps[64:128, 4, :].rearrange("p (b g d) -> p b g d", g=HP, d=HD)).then_inc(s_v1, 1)
                    if a == 1:
                        for k in range(CP):
                            t = c * CP + k
                            wait(dve, s_relp, t + 1)
                            if k >= 2 or not isinstance(c, int) or c >= 1:
                                dve.wait_ge(s_rw[k % 2], (c * 2 + k // 2) * 16)
                            v.tensor_copy(relst[:, k % 2, 512:1024], ps[:, 7, :]).then_inc(s_re1, 1)
                chunks(dve, project)

                def attend(t, u, i):
                    if live(t, u, i, 0):
                        z = u % 2
                        wait(dve, s_qk, t + t0 + 1)
                        if a == 1:
                            wait(dve, s_p, t - 1)
                            k = u // 4 + 1 if i is None else None
                            dve.wait_ge(s_rl[u % 4], 32 * (i * 2 + u // 4 + 1))
                            v.tensor_tensor(SS[:, z, :, :].rearrange("p h j -> p (h j)"),
                                            ps[:, 2 * z:2 * z + 2, :].rearrange("p k c -> p (k c)"),
                                            relsh[:, u % 4, :], ALU.add).then_inc(s_add, 1)
                            wait(dve, s_add, t + 1)
                            wait(dve, s_sub, t - 1)
                            v.tensor_reduce(negm[:, z, :], SS[:, z, :, :], AX.X, ALU.max, negate=True).then_inc(s_mx, 1)
                        else:
                            wait(dve, s_sub, t + t0 - 1)
                            v.tensor_reduce(negm[:, z, :],
                                            ps[:, 2 * z:2 * z + 2, :].rearrange("p k (h j) -> p (k h) j", j=S),
                                            AX.X, ALU.max, negate=True).then_inc(c_dve[2], 1)
                            wait(dve, c_dve[2], 2 * t + 1)
                            v.tensor_copy(nhi[:, z, :], negm[:, z, :]).then_inc(c_dve[2], 1)
                            wait(dve, c_dve[2], 2 * t + 2)
                            v.tensor_tensor(nlo[:, z, :], negm[:, z, :], nhi[:, z, :], ALU.subtract).then_inc(s_mx, 1)
                    if live(t, u, i, 2):
                        wait(dve, s_t, 2 * (t + t0 - 1))
                        wait(dve, s_pv, t + t0 - 3)
                        v.tensor_copy(PT[:, u % 2, 512:1024], ps[:, 5, :]).then_inc(s_e1, 1)
                    if live(t, u, i, 3):
                        wait(dve, s_pv, t + t0 - 2)
                        O = ps[:, 6, 0:HP * 2 * VW].rearrange("p (g b w) -> p g b w", b=2, w=VW)
                        v.reciprocal(rden[:, :].rearrange("p (g h) -> p g h", h=2),
                                     O[:, :, 0, 2 * HD:VW]).then_inc(c_dve[3], 1)
                        dve.wait_ge(c_dve[3], t + t0 - 2)
                        k = (u - 3) % 4
                        cs = ((u - 3) % 8) // 4
                        if k == 0 and (a == 2 or not isinstance(t, int) or t >= 11):
                            if isinstance(t, int):
                                cn = (t + t0 - 3) // 4
                            else:
                                cn = i * 2 + (u - 3) // 4 + (a - 1) * NCH
                            wait(dve, s_ot, cn - 1)
                        for par in range(2):
                            q = slice(par * 64, par * 64 + 64)
                            v.tensor_tensor(on[q, cs, k, :].rearrange("p (g h d) -> p g h d", h=2, d=HD),
                                            O[q, :, par, 0:2 * HD].rearrange("p g (h d) -> p g h d", d=HD),
                                            rden[q, :].rearrange("p (g h) -> p g h", h=2).unsqueeze(3)
                                            .broadcast_to([64, HP, 2, HD]), ALU.mult).then_inc(s_on, 1)
                    if u % 4 == 0 and live(t, u, i, 5):
                        if isinstance(t, int):
                            cl = (t - 8) // 4 if t >= 8 else t // 4 - 2
                            cl = t // 4 - 2
                        else:
                            cl = i * 2 + u // 4 - 2
                        if isinstance(cl, int) and cl < 0:
                            return
                        wait(dve, s_wo, cl + n0 + 1)
                        xs = X[:, bass.ds(cl * CP, CP), :].rearrange("p q d -> p (q d)")
                        v.tensor_tensor(xs, xs, ps[:, 7, :], ALU.add).then_inc(s_x, 1)
                steps(dve, attend, 5)

            dve.wait_ge(s_x, 2 * NCH)
            chf = Chain(c_dve[4], 2 * 11)

            def ffn(c, h, i):
                if h == 0:
                    chf.at(i)
                norm(c + 2 * NCH, c, chf)
                wait(dve, s_lgp, c + 1)
                chf.link(v.tensor_copy(lg[:, :, :].rearrange("p q e -> p (q e)"), ps[:, 1, 0:CP * E]))
                v.memset(idle[:, :], 0.0)
                for k in range(CP):
                    last = v.max(mx[:, k, :], lg[:, k, :])
                chf.link(last)
                wait(dve, s_eg, c)
                v.tensor_tensor(dgate[:, :], mx[:, :, 1], mx[:, :, 0], ALU.subtract).then_inc(s_dg, 1)
                for k in range(CP):
                    last = v.max_index(ix[:, k, :], mx[:, k, :], lg[:, k, :])
                chf.link(last)
                chf.link(v.tensor_copy(ixf[:, :, :], ix[:, :, 0:TOPK]))
                io = iota8[:, :].unsqueeze(1).broadcast_to([128, CP, E])
                for r in range(TOPK):
                    last = v.tensor_tensor(eq[:, r, :, :], io, ixf[:, :, r:r + 1].broadcast_to([128, CP, E]),
                                           ALU.is_equal)
                chf.link(last)
                wait(dve, s_eg, c + 1)
                chf.link(v.tensor_scalar(gate[:, 1, :], egate[:, :], 1.0, None, ALU.add))
                chf.link(v.reciprocal(gate[:, 0, :], gate[:, 1, :]))
                chf.link(v.tensor_tensor(gate[:, 1, :], gate[:, 0, :], egate[:, :], ALU.mult))
                for r in range(TOPK):
                    last = v.tensor_tensor(eq[:, r, :, :], eq[:, r, :, :],
                                           gate[:, r, :].unsqueeze(2).broadcast_to([128, CP, E]), ALU.mult)
                chf.link(last)
                wait(dve, s_cfp, c)
                v.tensor_tensor(coef[:, :, :], eq[:, 0, :, :], eq[:, 1, :, :], ALU.add).then_inc(s_cf, 1)
                for k in range(NC4):
                    wait(dve, s_g, 4 * c + k + 1)
                    wait(dve, s_hb, 4 * c + k + 1)
                    wait(dve, s_yo, 4 * c + k - 1)
                    v.tensor_tensor(hw[:, k % 2, :], ps[:, 3 if k % 2 else 6, :], hg[:, k % 2, :],
                                    ALU.mult).then_inc(s_hw, 1)
                wait(dve, s_yo, 4 * c + 4)
                if not isinstance(c, int) or c >= 2:
                    dve.wait_ge(s_out[h], 16 * i)
                v.scalar_tensor_tensor(yst[:, h, :, :].rearrange("p q d -> p (q d)"), ps[:, 7, :], LORA,
                                       X[:, bass.ds(c * CP, CP), :].rearrange("p q d -> p (q d)"),
                                       ALU.mult, ALU.add).then_inc(s_y, 1)
            chunks(dve, ffn)

        @block.tensor
        def _(pe):
            m = nc.tensor
            pe.wait_ge(s_cst, 8)
            pe.wait_ge(s_w, 16 * NWDMA)

            def transpose_chunk(bank, src, n, done_in, s_ready):
                for k in range(CP):
                    last = m.transpose(ps[:, bank, k * 128:(k + 1) * 128], src[:, k, :], ident[:, :])
                last.then_inc(s_ready, 1)

            for a in (1, 2):
                n0 = (a - 1) * NCH
                t0 = (a - 1) * NPAIR
                if a == 2:
                    pe.wait_ge(s_x, NCH)

                def project(c, h, i):
                    n = c + n0
                    wait(pe, s_xn, n + 1)
                    wait(pe, s_xnT, n)
                    transpose_chunk(0, xn, n, None, s_xtp)
                    src = xnT
                    if a == 2:
                        pe.wait_ge(s_ctx[h], 16 * (i + 1))
                        wait(pe, s_cxT, c)
                        transpose_chunk(1, cx[:, h, :, :], n, None, s_ctp)
                        src = cxT
                    wait(pe, s_xnT, n + 1)
                    wait(pe, s_qf, 2 * n)
                    wait(pe, s_kf, 4 * n - 2)
                    m.matmul(ps[:, 2, :], wt["q", a][:, :], xnT[:, h, :], start=True, stop=True)
                    if a == 2:
                        wait(pe, s_cxT, c + 1)
                    m.matmul(ps[:, 3, :], wt["k", a][:, :], src[:, h, :], start=True, stop=True).then_inc(s_qkp, 1)
                    wait(pe, s_v0, n)
                    wait(pe, s_v1, n)
                    for z in range(2):
                        o = ps[64 * z:64 * z + 64, 4, :]
                        bv = brow[0:1, 2 * a - 2, :].rearrange("p (g h d) -> p g h d", h=2, d=HD)[:, :, z, :]
                        wv = wt["v", a][:, :].rearrange("p (g h d) -> p g h d", h=2, d=HD)[:, :, z, :]
                        for k in range(2 * CP):
                            m.matmul(o[:, k * 64:(k + 1) * 64], ones[0:1, 0:64], bv, start=(k == 0), stop=False,
                                     skip_group_check=True)
                            last = m.matmul(o[:, k * 64:(k + 1) * 64], src[:, h, k * S:(k + 1) * S], wv,
                                            start=False, stop=(k == 2 * CP - 1), skip_group_check=True)
                    last.then_inc(s_vp, 1)
                    if a == 1:
                        pe.wait_ge(s_qf, 2 * (c + 1) - 1)
                        for k in range(CP):
                            t = c * CP + k
                            wait(pe, s_re0, t)
                            wait(pe, s_re1, t)
                            lhs = qk[:, 0, :].rearrange("p (c q) -> p q c", q=CP)[:, k, :]
                            for z in range(2):
                                last = m.matmul(ps[:, 6 + z, :], lhs, relw[:, z * HP:(z + 1) * HP, :],
                                                start=True, stop=True)
                            last.then_inc(s_relp, 1)
                chunks(pe, project)
                pe.wait_ge(s_v0, n0 + NCH)
                pe.wait_ge(s_v1, n0 + NCH)
                pe.wait_ge(s_qf, 2 * (n0 + NCH))
                pe.wait_ge(s_kf, 4 * (n0 + NCH))
                if a == 1:
                    pe.wait_ge(s_re0, NPAIR)
                    pe.wait_ge(s_re1, NPAIR)

                def attend(t, u, i):
                    if live(t, u, i, 0):
                        z = u % 2
                        if u % 4 == 0:
                            pe.wait_ge(s_st[u // 4], 16 * 4 * NPROD * (i + 1 + (a - 1) * NCH // 2))
                        wait(pe, s_add if a == 1 else s_p, t + (0 if a == 1 else t0) - 1)
                        for b in range(2):
                            if a == 1:
                                m.matmul(ps[:, 2 * z + b, :], identb[:, :],
                                         maskneg[:, :].unsqueeze(1).broadcast_to([128, HP, S]),
                                         start=True, stop=False, skip_group_check=True)
                            for h in range(HP):
                                k = (u % 4) * S
                                last = m.matmul(ps[:, 2 * z + b, h * S:(h + 1) * S],
                                                Qst[0:KROWS, u // 4, b * HP + h, :, :]
                                                .rearrange("p b (i q) -> p q (b i)", q=CP)[:, u % 4, :],
                                                Kst[0:KROWS, u // 4, b * HP + h, k:k + S],
                                                start=(a == 2 and h == 0), stop=(a == 1 and h == HP - 1),
                                                skip_group_check=True)
                        last.then_inc(s_qk, 1)
                    if a == 2 and live(t, u, i, 1):
                        z = (u - 1) % 2
                        wait(pe, s_mx, t + t0)
                        for b in range(2):
                            for part in (nhi, nlo):
                                last = m.matmul(ps[:, 2 * z + b, :], identb[:, :],
                                                part[:, z, b * HP:(b + 1) * HP].unsqueeze(2).broadcast_to([128, HP, S]),
                                                start=False, stop=(part is nlo), skip_group_check=True)
                        last.then_inc(s_sub, 1)
                    if live(t, u, i, 2):
                        z = u % 2
                        wait(pe, s_p, t + t0 - 1)
                        for b in range(2):
                            wait(pe, (s_e0, s_e1)[b], t + t0 - 2)
                            for k in range(4):
                                last = m.transpose(ps[:, 4 + b, k * 128:(k + 1) * 128],
                                                   P[:, z, (b * 4 + k) * 128:(b * 4 + k + 1) * 128], ident[:, :])
                            last.then_inc(s_t, 1)
                    if live(t, u, i, 3):
                        z = (u - 3) % 2
                        wait(pe, s_e0, t + t0 - 2)
                        wait(pe, s_e1, t + t0 - 2)
                        wait(pe, s_on, 2 * (t + t0 - 3))
                        for g in range(HP):
                            last = m.matmul(ps[:, 6, g * 2 * VW:(g + 1) * 2 * VW], PT[:, z, g * 128:(g + 1) * 128],
                                            V[:, bass.ds((t - 3) * 2, 2), g, :], start=True, stop=True)
                        last.then_inc(s_pv, 1)
                    if u % 4 == 3 and live(t, u, i, 7):
                        cs = ((u - 7) % 8) // 4
                        if isinstance(t, int):
                            cn = (t + t0 - 3) // 4
                        else:
                            cn = i * 2 + (u - 3) // 4 + (a - 1) * NCH
                        wait(pe, s_on, 8 * cn)
                        wait(pe, s_x, cn - 1)
                        transpose_chunk(7, on[:, cs, :, :], None, None, s_ot)
                    if u % 4 == 0 and live(t, u, i, 5):
                        if isinstance(t, int):
                            cn = t // 4 - 1 + n0
                            if t < 8:
                                return
                        else:
                            cn = i * 2 + u // 4 - 1 + n0
                        wait(pe, s_onT, cn)
                        bo = brow[0:1, 2 * a - 1, :].unsqueeze(1).broadcast_to([1, CP, D])
                        m.matmul(ps[:, 7, :], ones[0:1, :], bo, start=True, stop=False, skip_group_check=True)
                        for k in range(CP):
                            last = m.matmul(ps[:, 7, k * 128:(k + 1) * 128], onT[:, k * 128:(k + 1) * 128],
                                            wt["o", a][:, :], start=False, stop=(k == CP - 1), skip_group_check=True)
                        last.then_inc(s_wo, 1)
                steps(pe, attend, 5)

            pe.wait_ge(s_x, 2 * NCH)

            def ffn(c, h, i):
                n = c + 2 * NCH
                wait(pe, s_xn, n + 1)
                wait(pe, s_xnT, n)
                transpose_chunk(0, xn, n, None, s_xtp)
                wait(pe, s_xnT, n + 1)
                wait(pe, s_dg, c)
                m.matmul(ps[:, 1, 0:CP * E], ones[0:1, :], bg[0:1, :, :], start=True, stop=False,
                         skip_group_check=True)
                for k in range(CP):
                    last = m.matmul(ps[:, 1, k * E:(k + 1) * E], xnT[:, h, k * 128:(k + 1) * 128], wg[:, :],
                                    start=False, stop=(k == CP - 1), skip_group_check=True)
                last.then_inc(s_lgp, 1)

                def up(k):
                    wait(pe, s_g, 4 * c + k - 1)
                    m.matmul(ps[:, 4 + k % 2, :], w1[:, k * 128:(k + 1) * 128], xnT[:, h, :],
                             start=True, stop=True).then_inc(s_h, 1)
                up(0)
                up(1)
                wait(pe, s_cf, c + 1)
                wait(pe, s_cfT, c)
                for k in range(CP):
                    last = m.transpose(ps[0:E, 2, k * 128:(k + 1) * 128], coef[:, k, :], ident[:, :])
                last.then_inc(s_cfp, 1)
                wait(pe, s_cfT, c + 1)
                for k in range(NC4):
                    wait(pe, s_hw, 4 * c + k - 1)
                    m.matmul(ps[:, 3 if k % 2 else 6, :], sel[:, k * 128:(k + 1) * 128], coefT[:, :],
                             start=True, stop=True).then_inc(s_hb, 1)
                    if k + 2 < NC4:
                        up(k + 2)
                    wait(pe, s_hw, 4 * c + k + 1)
                    if k == 0:
                        wait(pe, s_y, c)
                    for q in range(CP):
                        last = m.matmul(ps[:, 7, q * 128:(q + 1) * 128], hw[:, k % 2, q * 128:(q + 1) * 128],
                                        w2[:, k, :], start=(k == 0 and q == 0), stop=(k == NC4 - 1),
                                        skip_group_check=True)
                    last.then_inc(s_yo, 1)
            chunks(pe, ffn)


def kernel(**inputs):
    import numpy as np
    import concourse.bacc as bacc
    from concourse.bass_utils import run_bass_kernel_spmd

    nc = bacc.Bacc("TRN2", target_bir_lowering=False, num_devices=1)
    arrays = {}

    def put(name, a):
        a = np.ascontiguousarray(a)
        arrays["in_" + name] = a
        return nc.dram_tensor("in_" + name, a.shape, mybir.dt.from_np(a.dtype), kind="ExternalInput").ap()

    g = {k: np.asarray(v) for k, v in inputs.items()}
    x = put("x", g["x"])
    c = put("ctx", g["ctx_1024"])
    w = {}
    for n in "qkvo":
        w[f"W{n}1"] = put(f"W{n}1", g[f"L0_attn_W{n}"])
        w[f"W{n}2"] = put(f"W{n}2", g[f"L0_xattn_W{n}"].T)
        shape = (D, 1) if n in "qk" else (1, D)
        w[f"b{n}1"] = put(f"b{n}1", g[f"L0_attn_b{n}"].reshape(shape))
        w[f"b{n}2"] = put(f"b{n}2", g[f"L0_xattn_b{n}"].reshape(shape))
    w["rel"] = put("rel", g["L0_attn_rel_key"][-S:].T)
    w["Wg"] = put("Wg", g["L0_ffn_Wg"].T)
    w["bg"] = put("bg", g["L0_ffn_bg"].reshape(1, E))
    w["W1"] = put("W1", g["L0_ffn_W1"].reshape(E * R, D).T)
    w["W2"] = put("W2", g["L0_ffn_W2"].transpose(0, 2, 1).reshape(E * R, D))
    out = nc.dram_tensor("out", (B, S, D), F32, kind="ExternalOutput").ap()
    build(nc, x, c, w, out)
    r = run_bass_kernel_spmd(nc, [arrays], core_ids=[0])
    return r.results[0]["out"]
```

```python
import concourse.bass as bass
import concourse.mybir as mybir
from concourse.alu_op_type import AluOpType as ALU

F32 = mybir.dt.float32
BF16 = mybir.dt.bfloat16
U32 = mybir.dt.uint32
ACT = mybir.ActivationFunctionType
AX = mybir.AxisListType

B, S, D = 64, 64, 128
H, HD = 16, 8
HP = H // 2
NPAIR = B // 2
CP = 4
NCH = NPAIR // CP
CT = CP * 128
HALF = CT // 2
SC = H * S
E, R = 8, 64
NC4 = E * R // 128
TOPK = 2
LORA = 2.0
EPS = 1e-5
NEG = -1.0e30
NSPLIT = 3
NPROD = 6
RUNS = ((0, 3, 0), (3, 2, 1), (5, 1, 2))
KROWS = 64 + NPROD * HD
VW = 18


def build(nc, x_in, ctx_in, w, out):
    from contextlib import ExitStack
    ctx = ExitStack()
    with ctx:
        def sb(name, shape, dt=F32):
            return ctx.enter_context(nc.sbuf_tensor(name, shape, dt))

        def sem(name):
            return ctx.enter_context(nc.semaphore(name))

        X = sb("X", [128, NPAIR, D])
        ident = sb("ident", [128, 128])
        identb = sb("identb", [128, 128], BF16)
        maskneg = sb("maskneg", [128, S])
        ones = sb("ones", [1, 128])
        wall = sb("wall", [128, 2, 4, D])
        wt = {(n, a): wall[:, a - 1, k, :] for a in (1, 2) for k, n in enumerate("qkvo")}
        bcol = sb("bcol", [128, 2, 3])
        brow = sb("brow", [1, 2, D])
        borep = sb("borep", [128, 2, D])
        relrep = sb("relrep", [128, S])
        headrow = sb("headrow", [128, H])
        relw = sb("relw", [128, H, S])
        wg = sb("wg", [128, E])
        bg = sb("bg", [1, E])
        w1 = sb("w1", [128, E * R])
        w2 = sb("w2", [128, NC4, D])
        selw = sb("selw", [NSPLIT * E, E * R])
        selb = sb("selb", [NSPLIT * E, E * R], BF16)
        iota8 = sb("iota8", [128, E])
        nhalf = sb("nhalf", [128, CP])
        ecst = sb("ecst", [128, CP])
        Qst = sb("Qst", [128, 2, H, 2, HALF], BF16)
        Kst = sb("Kst", [128, 2, H, HALF], BF16)
        V = sb("V", [128, NPAIR * 2, HP, VW])
        st6 = sb("st6", [128, CP, 6])
        mv = sb("mv", [128, CP, 2])
        veps = sb("veps", [128, CP])
        rstd = sb("rstd", [128, CP])
        xn = sb("xn", [128, CP, D])
        xnT = sb("xnT", [128, 2, CT])
        qk = sb("qk", [128, 2, CT])
        qkr = sb("qkr", [128, 2, CT])
        parts = sb("parts", [128, 2, 2, NSPLIT, CT], BF16)
        relst = sb("relst", [128, 2, SC + 1])
        relsh = sb("relsh", [128, 4, SC])
        cx = relst[:, 0, 0:SC].rearrange("p (s q d) -> p s q d", s=2, d=D)
        cxT = relst[:, 1, 0:SC].rearrange("p (s c) -> p s c", s=2)
        SS = sb("SS", [128, 2, H, S])
        negm = sb("negm", [128, 2, H])
        P = sb("P", [128, 2, SC])
        PT = sb("PT", [128, 2, SC])
        idle = sb("idle", [128, 1])
        rden = sb("rden", [128, H])
        on = sb("on", [128, 2, CP, D])
        onT = sb("onT", [128, CT])
        lg = sb("lg", [128, CP, E])
        mx = sb("mx", [128, CP, 8])
        ix = sb("ix", [128, CP, 8], U32)
        ixf = sb("ixf", [128, CP, TOPK])
        dgate = sb("dgate", [128, CP])
        egate = sb("egate", [128, CP])
        gate = sb("gate", [128, TOPK, CP])
        eq = sb("eq", [128, TOPK, CP, E])
        coef = sb("coef", [128, CP, E])
        coefr = sb("coefr", [128, CP, E])
        coefp = sb("coefp", [128, CP, NSPLIT, E], BF16)
        coefT = sb("coefT", [NSPLIT * E, CT], BF16)
        hg = relsh[:, 0, :].rearrange("p (s c) -> p s c", s=2)
        hw = relsh[:, 1, :].rearrange("p (s c) -> p s c", s=2)
        yst = relsh[:, 2, :].rearrange("p (s q d) -> p s q d", s=2, d=D)

        partD = nc.dram_tensor("parts_scratch", [2, NCH, 2, NSPLIT, 2, HD, H, HALF], BF16, kind="Internal")
        PART = 2 * 128 * HALF
        relD = nc.dram_tensor("rel_scratch", [NPAIR, 128, SC + 1], F32, kind="Internal")

        ps = ctx.enter_context(nc.psum_tensor("ps", [128, 8, 512], F32))

        s_x0 = sem("s_x0")
        s_xr = sem("s_xr")
        s_w1 = sem("s_w1")
        s_w2 = sem("s_w2")
        s_rel = sem("s_rel")
        s_head = sem("s_head")
        s_relw = sem("s_relw")
        s_bop = sem("s_bop")
        s_bo = sem("s_bo")
        s_xb = sem("s_xb")
        s_selb = sem("s_selb")
        s_ms = sem("s_ms")
        s_sz = sem("s_sz")
        s_vz = sem("s_vz")
        s_cst = sem("s_cst")
        s_ctx = [sem(f"s_ctx{h}") for h in range(2)]
        s_stat = sem("s_stat")
        s_rstd = sem("s_rstd")
        s_xn = sem("s_xn")
        s_xtp = sem("s_xtp")
        s_xnT = sem("s_xnT")
        s_ctp = sem("s_ctp")
        s_cxT = sem("s_cxT")
        s_qkp = sem("s_qkp")
        s_qf = sem("s_qf")
        s_kf = sem("s_kf")
        s_r = sem("s_r")
        s_p2 = sem("s_p2")
        s_q3 = sem("s_q3")
        s_k3 = sem("s_k3")
        s_pw = [sem(f"s_pw{h}") for h in range(2)]
        s_vp = sem("s_vp")
        s_v0 = sem("s_v0")
        s_v1 = sem("s_v1")
        s_relp = sem("s_relp")
        s_re0 = sem("s_re0")
        s_rm = sem("s_rm")
        s_re1 = sem("s_re1")
        s_rw = [sem(f"s_rw{h}") for h in range(2)]
        s_st = [sem(f"s_st{h}") for h in range(2)]
        s_rl = [sem(f"s_rl{h}") for h in range(4)]
        s_qk = sem("s_qk")
        s_add = sem("s_add")
        s_sc = sem("s_sc")
        s_mx = sem("s_mx")
        s_sub = sem("s_sub")
        s_p = sem("s_p")
        s_t = sem("s_t")
        s_e0 = sem("s_e0")
        s_e1 = sem("s_e1")
        s_pv = sem("s_pv")
        s_on = sem("s_on")
        s_ot = sem("s_ot")
        s_onT = sem("s_onT")
        s_wo = sem("s_wo")
        s_x = sem("s_x")
        c_dve = [sem(f"c_dve{n}") for n in range(5)]
        s_lgp = sem("s_lgp")
        s_dg = sem("s_dg")
        s_eg = sem("s_eg")
        s_cf = sem("s_cf")
        s_cfp = sem("s_cfp")
        s_cfT = sem("s_cfT")
        s_h = sem("s_h")
        s_hb = sem("s_hb")
        s_g = sem("s_g")
        s_hw = sem("s_hw")
        s_y = sem("s_y")
        s_yo = sem("s_yo")
        s_out = [sem(f"s_out{h}") for h in range(2)]

        NW1, NW2 = 16 * 3, 16 * 6

        def wait(eng, s, n):
            if isinstance(n, int) and n <= 0:
                return
            eng.wait_ge(s, n)

        def chunks(eng, body):
            for h in range(2):
                body(h, h, 0)
            with eng.Fori(1, NCH // 2) as i:
                for h in range(2):
                    body(i * 2 + h, h, i)

        def pipe(eng, body):
            body((0, 0, 0), None)
            body((1, 1, 0), (0, 0, 0))
            with eng.Fori(1, NCH // 2) as i:
                body((i * 2, 0, i), (i * 2 - 1, 1, i - 1))
                body((i * 2 + 1, 1, i), (i * 2, 0, i))
            body(None, (NCH - 1, 1, NCH // 2 - 1))

        def steps(eng, body, last):
            for u in range(8):
                body(u, u, 0)
            with eng.Fori(1, NPAIR // 8) as i:
                for u in range(8):
                    body(i * 8 + u, u, i)
            for u in range(last):
                body(NPAIR + u, u, None)

        def live(t, u, i, lag):
            if i is None:
                return u - lag < 0
            return not isinstance(t, int) or t >= lag

        def slot2(u):
            return u % 2

        RELBANK = ((6, 7), (1, 5))

        block = ctx.enter_context(nc.Block())

        @block.sync
        def _(sp):
            xv = x_in.rearrange("(q b) s d -> (b s) q d", b=2)
            sp.dma_start(X[:, 0:CP, :], xv[:, 0:CP, :]).then_inc(s_x0, 16)
            sp.dma_start(wall[:, 0, :, :], w["W"][0]).then_inc(s_w1, 16)
            sp.dma_start(bcol[:, :, :], w["bcol"]).then_inc(s_w1, 16)
            sp.dma_start(brow[:, :, :], w["brow"]).then_inc(s_w1, 16)
            sp.dma_start(relrep[:, :], bass.AP(w["rel"].tensor, 0, [[S, HD], [0, H], [1, S]])).then_inc(s_rel, 16)
            sp.dma_start(X[:, CP:NPAIR, :], xv[:, CP:NPAIR, :]).then_inc(s_xr, 16)
            sp.dma_start(wall[:, 1, :, :], w["W"][1]).then_inc(s_w2, 16)
            sp.dma_start(wg[:, :], w["Wg"]).then_inc(s_w2, 16)
            sp.dma_start(bg[:, :], w["bg"]).then_inc(s_w2, 16)
            sp.dma_start(w1[:, :], w["W1"]).then_inc(s_w2, 16)
            sp.dma_start(w2[:, :, :], w["W2"].rearrange("(c p) d -> p c d", p=128)).then_inc(s_w2, 16)
            sp.dma_start(selw[:, :], w["sel"]).then_inc(s_w2, 16)

            for a in (1, 2):
                n0 = (a - 1) * NCH

                def load_stack(c, h):
                    wait(sp, s_qk, (c - 1) * CP + (a - 1) * NPAIR)
                    base = ((a - 1) * NCH + c) * 2 * NSPLIT * PART
                    for par in range(2):
                        for m0, nm, part in RUNS:
                            rows = slice(64 * par + m0 * HD, 64 * par + (m0 + nm) * HD)
                            first = base + part * PART + par * PART // 2
                            sp.dma_start(Qst[rows, h, :, par, :],
                                         bass.AP(partD, first, [[0, nm], [H * HALF, HD], [1, H * HALF]])
                                         ).then_inc(s_st[h], 16)
                            first = base + NSPLIT * PART + par * PART // 2
                            sp.dma_start(Kst[rows, h, :, :],
                                         bass.AP(partD, first, [[PART, nm], [H * HALF, HD], [1, H * HALF]])
                                         ).then_inc(s_st[h], 16)

                def load_rel(t, k):
                    wait(sp, s_add, t - 3)
                    src = bass.AP(relD, t * 128 * (SC + 1) + (S - 1), [[64 * (SC + 1), 2], [SC, 64], [1, SC]])
                    sp.dma_start(relsh[:, k, :], src).then_inc(s_rl[k], 16)

                def project(lead, follow):
                    if not follow:
                        return
                    c, h, k = follow
                    wait(sp, s_q3, c + 1 + n0)
                    wait(sp, s_k3, c + 1 + n0)
                    for z in range(2):
                        sp.dma_start(
                            bass.AP(partD, (((a - 1) * NCH + c) * 2 + z) * NSPLIT * PART,
                                    [[HALF, 128], [128 * HALF, NSPLIT * 2], [1, HALF]]),
                            parts[:, h, z, :, :].rearrange("p s (b c) -> p (s b) c", b=2)).then_inc(s_pw[h], 16)
                    if a == 1:
                        for r in range(CP):
                            t = c * CP + r
                            wait(sp, s_rm, t + 1)
                            wait(sp, s_re1, t + 1)
                            sp.dma_start(bass.AP(relD, t * 128 * (SC + 1), [[SC + 1, 128], [1, SC + 1]]),
                                         relst[:, r % 2, :]).then_inc(s_rw[r % 2], 16)
                    if isinstance(c, int) and c == 0:
                        if a == 1:
                            sp.wait_ge(s_sz, 2)
                        sp.wait_ge(s_pw[h], 32 * (n0 // 2 + 1))
                        load_stack(c, h)
                        if a == 1:
                            for q in range(2):
                                sp.wait_ge(s_rw[q], 32)
                            for r in range(CP):
                                load_rel(r, r)
                pipe(sp, project)

                for h in range(2):
                    sp.wait_ge(s_pw[h], 32 * (NCH // 2) * a)
                load_stack(1, 1)
                if a == 1:
                    for h in range(2):
                        sp.wait_ge(s_rw[h], 16 * (NPAIR // 2))

                def attend(c, h):
                    if a == 1:
                        for r in range(CP):
                            load_rel((c + 1) * CP + r, r)
                    load_stack(c + 2, h)
                with sp.Fori(0, NCH // 2 - 1) as i:
                    for h in range(2):
                        attend(i * 2 + h, h)
                if a == 1:
                    for r in range(CP):
                        load_rel((NCH - 1) * CP + r, r)

            def store(c, h, i):
                wait(sp, s_y, c + 1)
                outv = out.rearrange("(q b) s d -> (b s) q d", b=2)
                sp.dma_start(outv[:, bass.ds(c * CP, CP), :], yst[:, h, :, :]).then_inc(s_out[h], 16)
            chunks(sp, store)
            for h in range(2):
                sp.wait_ge(s_out[h], 16 * (NCH // 2))

        @block.gpsimd
        def _(pool):
            g = nc.gpsimd
            g.memset(ident[:, :], 0.0).then_inc(s_ms, 1)
            g.memset(maskneg[:, :], 0.0).then_inc(s_ms, 1)
            g.memset(ones[:, :], 1.0).then_inc(s_ms, 1)
            g.memset(nhalf[:, :], -0.5).then_inc(s_ms, 1)
            g.memset(ecst[:, :], 2.718281828459045).then_inc(s_ms, 1)
            g.iota(iota8[:, :], pattern=[[1, E]], base=0, channel_multiplier=0,
                   allow_small_or_imprecise_dtypes=True).then_inc(s_ms, 1)
            pool.wait_ge(s_ms, 6)
            g.affine_select(out=ident[:, :], in_=ident[:, :], compare_op=ALU.not_equal, fill=1.0,
                            base=0, pattern=[[-1, 128]], channel_multiplier=1).then_inc(s_cst, 1)
            for par in range(2):
                pool.wait_ge(s_cst, 1 + par)
                v = maskneg[par * 64:par * 64 + 64, :]
                g.affine_select(out=v, in_=v, compare_op=ALU.is_ge, fill=NEG, base=1 - S,
                                pattern=[[1, S]], channel_multiplier=1).then_inc(s_cst, 1)
            pool.wait_ge(s_cst, 3)
            g.tensor_copy(identb[:, :], ident[:, :]).then_inc(s_cst, 1)
            g.memset(relst[:, :, SC:SC + 1], NEG).then_inc(s_cst, 1)

            def power(n):
                wait(pool, s_stat, n + 1)
                g.tensor_tensor(rstd[:, :], veps[:, :], nhalf[:, :], ALU.pow).then_inc(s_rstd, 1)

            for a in (1, 2):
                n0 = (a - 1) * NCH
                t0 = (a - 1) * NPAIR

                def project(lead, follow):
                    if lead:
                        c, h, k = lead
                        power(c + n0)
                        if a == 1 and isinstance(c, int) and c == 0:
                            g.memset(Qst[:, :, :, :, :].rearrange("p a b c d -> p (a b c d)").bitcast(F32),
                                     0.0).then_inc(s_sz, 1)
                            g.memset(Kst[:, :, :, :].rearrange("p a b c -> p (a b c)").bitcast(F32),
                                     0.0).then_inc(s_sz, 1)
                    if follow:
                        c, h, k = follow
                        if a == 2 and not (isinstance(c, int) and c == 0):
                            third_part(c - 1, 1 - h)
                        wait(pool, s_qf, 2 * (c + n0 + 1))
                        wait(pool, s_q3, c + n0)
                        g.tensor_tensor(qkr[:, 0, :], qk[:, 0, :], parts[:, h, 0, 0, :],
                                        ALU.subtract).then_inc(s_r, 1)
                        if a == 1:
                            third_part(c, h)
                            for r in range(CP):
                                t = c * CP + r
                                wait(pool, s_re0, t + 1)
                                o = relst[:, r % 2, 0:512].rearrange("p (h j) -> p h j", j=S)
                                g.tensor_tensor(o, o, maskneg[:, :].unsqueeze(1).broadcast_to([128, HP, S]),
                                                ALU.add).then_inc(s_rm, 1)

                def third_part(c, h):
                    if a == 2:
                        wait(pool, s_kf, 4 * (c + n0) + 4)
                        g.tensor_tensor(parts[:, h, 1, 2, :], qkr[:, 1, :], parts[:, h, 1, 1, :],
                                        ALU.subtract).then_inc(s_k3, 1)
                    wait(pool, s_p2, c + n0 + 1)
                    g.tensor_tensor(parts[:, h, 0, 2, :], qkr[:, 0, :], parts[:, h, 0, 1, :],
                                    ALU.subtract).then_inc(s_q3, 1)
                pipe(pool, project)
                if a == 2:
                    third_part(NCH - 1, 1)

                def attend(t, u, i):
                    if u % 4 == 1:
                        wait(pool, s_xn, n0 + NCH)
                        if a == 1 and isinstance(t, int):
                            pool.wait_ge(s_bo, 1)
                        xs = X[:, bass.ds(t - 1, CP), :]
                        g.tensor_tensor(xs, xs, borep[:, a - 1:a, :].broadcast_to([128, CP, D]),
                                        ALU.add).then_inc(s_xb, 1)
                    wait(pool, s_mx, t + t0 + 1)
                    v = SS[:, slot2(u), :, :]
                    g.tensor_tensor(v, v, negm[:, slot2(u), :].unsqueeze(2).broadcast_to([128, H, S]),
                                    ALU.add).then_inc(s_sub, 1)
                steps(pool, attend, 0)

            def ffn(c, h, i):
                power(c + 2 * NCH)
                wait(pool, s_dg, c + 1)
                g.tensor_tensor(egate[:, :], ecst[:, :], dgate[:, :], ALU.pow).then_inc(s_eg, 1)
            chunks(pool, ffn)

        @block.scalar
        def _(act):
            A = nc.scalar
            ctxv = ctx_in.rearrange("(q b) s d -> (b s) q d", b=2)
            act.wait_ge(s_w1, NW1)
            for a in (1, 2):
                n0 = (a - 1) * NCH
                t0 = (a - 1) * NPAIR

                def project(lead, follow):
                    if lead and a == 2:
                        c, h, k = lead
                        wait(act, s_ctp, c - 1)
                        act.dma_start(cx[:, h, :, :], ctxv[:, bass.ds(c * CP, CP), :]).then_inc(s_ctx[h], 16)
                    if follow:
                        c, h, k = follow
                        wait(act, s_qkp, c + n0 + 1)
                        qv = ps[:, 2, :].rearrange("p (q b i) -> p b i q", b=2, i=S)
                        wait(act, s_r, c + n0)
                        if a == 1:
                            wait(act, s_relp, c * CP)
                        A.activation(qk[:, 0, :].rearrange("p (b i q) -> p b i q", b=2, i=S), qv,
                                     ACT.Identity, bias=bcol[:, a - 1, 0:1]).then_inc(s_qf, 1)
                        wait(act, s_pw[h], 32 * (k + n0 // 2))
                        wait(act, s_qf, 2 * (c + n0) + 1)
                        A.copy(parts[:, h, 0, 0, :], qk[:, 0, :]).then_inc(s_qf, 1)
                        if a == 1 and isinstance(c, int) and c == 0:
                            act.wait_ge(s_vz, 3)
                        wait(act, s_vp, c + n0 + 1)
                        A.copy(V[0:64, bass.ds(c * 2 * CP, 2 * CP), :, 0:HD],
                               ps[0:64, 4, :].rearrange("p (b g d) -> p b g d", g=HP, d=HD)).then_inc(s_v0, 1)

                    def second_part(c, h):
                        wait(act, s_r, c + n0 + 1)
                        A.copy(parts[:, h, 0, 1, :], qkr[:, 0, :]).then_inc(s_p2, 1)

                    def copy_relative(c, rs):
                        for r in rs:
                            t = c * CP + r
                            wait(act, s_relp, t + 1)
                            wait(act, s_rw[r % 2], (c * 2 + r // 2) * 16)
                            A.copy(relst[:, r % 2, 0:512], ps[:, RELBANK[r % 2][0], :]).then_inc(s_re0, 1)

                    if follow and a == 1:
                        second_part(follow[0], follow[1])
                        copy_relative(follow[0], (0, 1))
                    if lead:
                        c, h, k = lead
                        wait(act, s_xtp, c + n0 + 1)
                        wait(act, s_vp, c + n0 - 1)
                        A.copy(xnT[:, h, :], ps[:, 0, :]).then_inc(s_xnT, 1)
                        if a == 2:
                            wait(act, s_ctp, c + 1)
                            A.copy(cxT[:, h, :], ps[:, 1, :]).then_inc(s_cxT, 1)
                    if follow and a == 1:
                        copy_relative(follow[0], (2, 3))
                    if follow and a == 2:
                        second_part(follow[0], follow[1])
                if a == 2:
                    act.wait_ge(s_pv, NPAIR)
                pipe(act, project)

                def attend(t, u, i):
                    if a == 2 and live(t, u, i, 0):
                        wait(act, s_qk, t + t0 + 1)
                        wait(act, s_p, t + t0 - 1)
                        A.copy(SS[:, u % 2, :, :].rearrange("p h j -> p (h j)"),
                               ps[:, 2 * (u % 2):2 * (u % 2) + 2, :].rearrange("p k c -> p (k c)")).then_inc(s_sc, 1)
                    if live(t, u, i, 1):
                        v = (u - 1) % 2
                        wait(act, s_t, 2 * (t + t0 - 2))
                        wait(act, s_sub, t + t0)
                        A.activation(P[:, v, :], SS[:, v, :, :].rearrange("p h j -> p (h j)"), ACT.Exp,
                                     scale=HD ** -0.5 if a == 1 else 1.0).then_inc(s_p, 1)
                    if live(t, u, i, 2):
                        wait(act, s_t, 2 * (t + t0 - 2) + 1)
                        wait(act, s_pv, t + t0 - 3)
                        A.copy(PT[:, u % 2, 0:512], ps[:, 4, :]).then_inc(s_e0, 1)
                        if a == 1:
                            wait(act, s_t, 2 * (t + t0 - 1))
                            A.copy(PT[:, u % 2, 512:1024], ps[:, 5, :]).then_inc(s_e1, 1)
                    if u % 4 == 3 and live(t, u, i, 4):
                        c = (t + t0 - 3)
                        if isinstance(t, int):
                            cn = (t + t0 - 3) // 4
                        else:
                            cn = i * 2 + (u - 3) // 4 + (a - 1) * NCH
                        wait(act, s_ot, cn)
                        A.copy(onT[:, :], ps[:, 7, :]).then_inc(s_onT, 1)
                steps(act, attend, 4)

            act.wait_ge(s_w2, NW2)
            A.copy(selb[:, :], selw[:, :]).then_inc(s_selb, 1)

            def ffn(lead, follow):
                def ranks(c, r):
                    wait(act, s_h, 4 * c + r + 1)
                    wait(act, s_hw, 4 * c + r - 1)
                    A.activation(hg[:, r % 2, :], ps[:, 4 + r % 2, :], ACT.Gelu).then_inc(s_g, 1)
                if follow:
                    c = follow[0]
                    wait(act, s_cfp, c + 1)
                    wait(act, s_hb, 4 * c)
                    A.copy(coefT[:, :], ps[0:NSPLIT * E, 2, 0:CT // 2].bitcast(BF16)).then_inc(s_cfT, 1)
                    ranks(c, 0)
                    ranks(c, 1)
                if lead:
                    c, h, k = lead
                    wait(act, s_xtp, c + 2 * NCH + 1)
                    wait(act, s_h, 4 * (c - 1))
                    A.copy(xnT[:, h, :], ps[:, 0, :]).then_inc(s_xnT, 1)
                if follow:
                    ranks(follow[0], 2)
                    ranks(follow[0], 3)
            pipe(act, ffn)

        @block.vector
        def _(dve):
            v = nc.vector

            def clear_v():
                v.memset(V[:, :, :, :], 0.0).then_inc(s_vz, 1)
                dve.wait_ge(s_vz, 1)
                v.memset(V[0:64, :, :, 2 * HD:2 * HD + 1], 1.0).then_inc(s_vz, 1)
                v.memset(V[64:128, :, :, 2 * HD + 1:VW], 1.0).then_inc(s_vz, 1)

            class Chain:
                def __init__(self, s, per):
                    self.s, self.per, self.n, self.base = s, per, 0, 0

                def at(self, i):
                    self.base, self.n = (i * self.per if i is not None else self.base), 0 if i is not None else self.n

                def link(self, ins):
                    ins.then_inc(self.s, 1)
                    self.n += 1
                    dve.wait_ge(self.s, self.base + self.n)

            def stats(n, c, ch):
                if isinstance(n, int) and n <= 1:
                    dve.wait_ge((s_x0, s_xr)[n], 16)
                wait(dve, s_rstd, n)
                for k in range(CP):
                    last = v.bn_stats(st6[:, k, :], X[:, c * CP + k, :])
                ch.link(last)
                v.memset(idle[:, :], 0.0)
                for k in range(CP):
                    last = v.bn_aggr(mv[:, k, :], st6[:, k, :])
                ch.link(last)
                v.tensor_scalar(veps[:, :], mv[:, :, 1], EPS, None, ALU.add).then_inc(s_stat, 1)

            def norm(n, c):
                wait(dve, s_rstd, n + 1)
                wait(dve, s_xtp, n)
                for k in range(CP):
                    last = v.tensor_scalar(xn[:, k, :], X[:, c * CP + k, :], mv[:, k, 0:1], rstd[:, k:k + 1],
                                           ALU.subtract, ALU.mult)
                last.then_inc(s_xn, 1)

            for a in (1, 2):
                n0 = (a - 1) * NCH
                t0 = (a - 1) * NPAIR
                chp = Chain(c_dve[a - 1], 2 * 2)

                def project(lead, follow):
                    if lead:
                        c, h, k = lead
                        if h == 0:
                            chp.at(k)
                        if a == 2:
                            dve.wait_ge(s_x, c + 1)
                        stats(c + n0, c, chp)
                        if a == 2 or not follow:
                            norm(c + n0, c)
                    if follow:
                        c, h, k = follow
                        wait(dve, s_qkp, c + n0 + 1)
                        kv = ps[:, 3, :].rearrange("p (q b i) -> p b q i", b=2, i=S)
                        v.tensor_scalar(qk[:, 1, :].rearrange("p (b q i) -> p b q i", b=2, i=S), kv,
                                        bcol[:, a - 1, 1:2], None, ALU.add).then_inc(s_kf, 1)
                        wait(dve, s_pw[h], 32 * (k + n0 // 2))
                        dve.wait_ge(s_kf, 4 * (c + n0) + 1)
                        v.tensor_copy(parts[:, h, 1, 0, :], qk[:, 1, :]).then_inc(s_kf, 1)
                        dve.wait_ge(s_kf, 4 * (c + n0) + 2)
                        if a == 2:
                            wait(dve, s_k3, c + n0)
                        v.tensor_tensor(qkr[:, 1, :], qk[:, 1, :], parts[:, h, 1, 0, :],
                                        ALU.subtract).then_inc(s_kf, 1)
                        dve.wait_ge(s_kf, 4 * (c + n0) + 3)
                        v.tensor_copy(parts[:, h, 1, 1, :], qkr[:, 1, :]).then_inc(s_kf, 1)
                        if a == 1:
                            dve.wait_ge(s_kf, 4 * (c + n0) + 4)
                            v.tensor_tensor(parts[:, h, 1, 2, :], qkr[:, 1, :], parts[:, h, 1, 1, :],
                                            ALU.subtract).then_inc(s_k3, 1)
                    if lead:
                        c, h, k = lead
                        if a == 1 and isinstance(c, int) and c == 0:
                            clear_v()
                            dve.wait_ge(s_cst, 5)
                            v.tensor_reduce(headrow[:, :], ident[:, :].rearrange("p (d h) -> p h d", h=H), AX.X,
                                            ALU.add).then_inc(s_head, 1)
                            dve.wait_ge(s_head, 1)
                            dve.wait_ge(s_rel, 16)
                            v.tensor_tensor(relw[:, :, :], relrep[:, :].unsqueeze(1).broadcast_to([128, H, S]),
                                            headrow[:, :].unsqueeze(2).broadcast_to([128, H, S]),
                                            ALU.mult).then_inc(s_relw, 1)
                            dve.wait_ge(s_bop, 1)
                            v.tensor_copy(borep[:, :, :].rearrange("p a d -> p (a d)"),
                                          ps[:, 7, 0:2 * D]).then_inc(s_bo, 1)
                            dve.wait_ge(s_w1, NW1)
                    if follow:
                        c, h, k = follow
                        if lead and a == 1:
                            norm(lead[0], lead[0])
                        wait(dve, s_vp, c + n0 + 1)
                        v.tensor_copy(V[64:128, bass.ds(c * 2 * CP, 2 * CP), :, HD:2 * HD],
                                      ps[64:128, 4, :].rearrange("p (b g d) -> p b g d", g=HP, d=HD)).then_inc(s_v1, 1)
                        if a == 1:
                            for r in range(CP):
                                t = c * CP + r
                                wait(dve, s_relp, t + 1)
                                wait(dve, s_rw[r % 2], (c * 2 + r // 2) * 16)
                                v.tensor_tensor(relst[:, r % 2, 512:1024].rearrange("p (h j) -> p h j", j=S),
                                                ps[:, RELBANK[r % 2][1], :].rearrange("p (h j) -> p h j", j=S),
                                                maskneg[:, :].unsqueeze(1).broadcast_to([128, HP, S]),
                                                ALU.add).then_inc(s_re1, 1)
                if a == 2:
                    dve.wait_ge(s_pv, NPAIR)
                pipe(dve, project)

                def attend(t, u, i):
                    if live(t, u, i, 0):
                        z = u % 2
                        if a == 1:
                            wait(dve, s_qk, t + 1)
                            wait(dve, s_p, t - 1)
                            dve.wait_ge(s_rl[u % 4], 16 * (i * 2 + u // 4 + 1))
                            v.tensor_tensor(SS[:, z, :, :].rearrange("p h j -> p (h j)"),
                                            ps[:, 2 * z:2 * z + 2, :].rearrange("p k c -> p (k c)"),
                                            relsh[:, u % 4, :], ALU.add).then_inc(s_add, 1)
                            wait(dve, s_add, t + 1)
                            wait(dve, s_sub, t - 1)
                        else:
                            wait(dve, s_sc, t + 1)
                            wait(dve, s_sub, t + t0 - 1)
                        v.tensor_reduce(negm[:, z, :], SS[:, z, :, :], AX.X, ALU.max, negate=True).then_inc(s_mx, 1)
                    if a == 2 and live(t, u, i, 2):
                        wait(dve, s_t, 2 * (t + t0 - 1))
                        wait(dve, s_pv, t + t0 - 3)
                        v.tensor_copy(PT[:, u % 2, 512:1024], ps[:, 5, :]).then_inc(s_e1, 1)
                    if live(t, u, i, 3):
                        wait(dve, s_pv, t + t0 - 2)
                        O = ps[:, 6, 0:HP * 2 * VW].rearrange("p (g b w) -> p g b w", b=2, w=VW)
                        v.reciprocal(rden[:, :].rearrange("p (g h) -> p g h", h=2),
                                     O[:, :, 0, 2 * HD:VW]).then_inc(c_dve[3], 1)
                        dve.wait_ge(c_dve[3], t + t0 - 2)
                        k = (u - 3) % 4
                        cs = ((u - 3) % 8) // 4
                        if k == 0 and (a == 2 or not isinstance(t, int) or t >= 11):
                            if isinstance(t, int):
                                cn = (t + t0 - 3) // 4
                            else:
                                cn = i * 2 + (u - 3) // 4 + (a - 1) * NCH
                            wait(dve, s_ot, cn - 1)
                        for par in range(2):
                            q = slice(par * 64, par * 64 + 64)
                            v.tensor_tensor(on[q, cs, k, :].rearrange("p (g h d) -> p g h d", h=2, d=HD),
                                            O[q, :, par, 0:2 * HD].rearrange("p g (h d) -> p g h d", d=HD),
                                            rden[q, :].rearrange("p (g h) -> p g h", h=2).unsqueeze(3)
                                            .broadcast_to([64, HP, 2, HD]), ALU.mult).then_inc(s_on, 1)
                    if u % 4 == 0 and live(t, u, i, 5):
                        if isinstance(t, int):
                            cl = (t - 8) // 4 if t >= 8 else t // 4 - 2
                            cl = t // 4 - 2
                        else:
                            cl = i * 2 + u // 4 - 2
                        if isinstance(cl, int) and cl < 0:
                            return
                        wait(dve, s_xb, cl + n0 + 1)
                        wait(dve, s_wo, cl + n0 + 1)
                        xs = X[:, bass.ds(cl * CP, CP), :].rearrange("p q d -> p (q d)")
                        v.tensor_tensor(xs, xs, ps[:, 7, :], ALU.add).then_inc(s_x, 1)
                steps(dve, attend, 5)

            chf = Chain(c_dve[4], 2 * 15)

            def experts(c):
                wait(dve, s_lgp, c + 1)
                chf.link(v.tensor_copy(lg[:, :, :].rearrange("p q e -> p (q e)"), ps[:, 1, 0:CP * E]))
                v.memset(idle[:, :], 0.0)
                for k in range(CP):
                    last = v.max(mx[:, k, :], lg[:, k, :])
                chf.link(last)
                wait(dve, s_eg, c)
                v.tensor_tensor(dgate[:, :], mx[:, :, 1], mx[:, :, 0], ALU.subtract).then_inc(s_dg, 1)
                for k in range(CP):
                    last = v.max_index(ix[:, k, :], mx[:, k, :], lg[:, k, :])
                chf.link(last)

            def gates(c):
                chf.link(v.tensor_copy(ixf[:, :, :], ix[:, :, 0:TOPK]))
                io = iota8[:, :].unsqueeze(1).broadcast_to([128, CP, E])
                for r in range(TOPK):
                    last = v.tensor_tensor(eq[:, r, :, :], io, ixf[:, :, r:r + 1].broadcast_to([128, CP, E]),
                                           ALU.is_equal)
                chf.link(last)
                wait(dve, s_eg, c + 1)
                chf.link(v.tensor_scalar(gate[:, 1, :], egate[:, :], 1.0, None, ALU.add))
                chf.link(v.reciprocal(gate[:, 0, :], gate[:, 1, :]))
                chf.link(v.tensor_tensor(gate[:, 1, :], gate[:, 0, :], egate[:, :], ALU.mult))
                for r in range(TOPK):
                    last = v.tensor_tensor(eq[:, r, :, :], eq[:, r, :, :],
                                           gate[:, r, :].unsqueeze(2).broadcast_to([128, CP, E]), ALU.mult)
                chf.link(last)
                wait(dve, s_cfp, c)
                chf.link(v.tensor_tensor(coef[:, :, :], eq[:, 0, :, :], eq[:, 1, :, :], ALU.add))
                chf.link(v.tensor_copy(coefp[:, :, 0, :], coef[:, :, :]))
                chf.link(v.tensor_tensor(coefr[:, :, :], coef[:, :, :], coefp[:, :, 0, :], ALU.subtract))
                chf.link(v.tensor_copy(coefp[:, :, 1, :], coefr[:, :, :]))
                v.tensor_tensor(coefp[:, :, 2, :], coefr[:, :, :], coefp[:, :, 1, :], ALU.subtract).then_inc(s_cf, 1)

            def weight(c, k):
                wait(dve, s_g, 4 * c + k + 1)
                wait(dve, s_hb, 4 * c + k + 1)
                wait(dve, s_yo, 4 * c + k - 1)
                v.tensor_tensor(hw[:, k % 2, :], ps[:, 3 if k % 2 else 6, :], hg[:, k % 2, :],
                                ALU.mult).then_inc(s_hw, 1)

            def residual(c, h, k):
                wait(dve, s_yo, 4 * c + 4)
                wait(dve, s_out[h], 16 * k)
                v.scalar_tensor_tensor(yst[:, h, :, :].rearrange("p q d -> p (q d)"), ps[:, 7, :], LORA,
                                       X[:, bass.ds(c * CP, CP), :].rearrange("p q d -> p (q d)"),
                                       ALU.mult, ALU.add).then_inc(s_y, 1)

            def ffn(lead, follow):
                if lead:
                    c, h, k = lead
                    if h == 0:
                        chf.at(k)
                    dve.wait_ge(s_x, c + NCH + 1)
                    stats(c + 2 * NCH, c, chf)
                if follow:
                    c, h, k = follow
                    if not (isinstance(c, int) and c == 0):
                        residual(c - 1, 1 - h, k - (1 - h))
                if lead:
                    norm(lead[0] + 2 * NCH, lead[0])
                if follow:
                    weight(c, 0)
                    weight(c, 1)
                if lead:
                    experts(lead[0])
                if follow:
                    weight(c, 2)
                if lead:
                    gates(lead[0])
                if follow:
                    weight(c, 3)
            pipe(dve, ffn)
            residual(NCH - 1, 1, NCH // 2 - 1)

        @block.tensor
        def _(pe):
            m = nc.tensor
            pe.wait_ge(s_cst, 5)

            def output_biases():
                pe.wait_ge(s_w1, NW1)
                pe.wait_ge(s_w2, NW2)
                for a in (1, 2):
                    o = ps[:, 7, (a - 1) * D:a * D]
                    m.matmul(o, bcol[:, a - 1, 2:3].broadcast_to([128, 128]), wt["o", a], start=True, stop=False)
                    last = m.matmul(o, ones[0:1, :], brow[0:1, a - 1, :], start=False, stop=True)
                last.then_inc(s_bop, 1)

            def transpose_chunk(bank, src, s_ready):
                for k in range(CP):
                    last = m.transpose(ps[:, bank, k * 128:(k + 1) * 128], src[:, k, :], ident[:, :])
                last.then_inc(s_ready, 1)

            for a in (1, 2):
                n0 = (a - 1) * NCH
                t0 = (a - 1) * NPAIR
                if a == 2:
                    pe.wait_ge(s_add, NPAIR)
                    pe.wait_ge(s_e0, NPAIR)

                src = xnT if a == 1 else cxT

                def transposes(c, h, k):
                    n = c + n0
                    wait(pe, s_xn, n + 1)
                    wait(pe, s_xnT, n)
                    transpose_chunk(0, xn, s_xtp)
                    if a == 2:
                        pe.wait_ge(s_ctx[h], 16 * (k + 1))
                        wait(pe, s_cxT, c)
                        transpose_chunk(1, cx[:, h, :, :], s_ctp)

                def queries_keys_values(c, h):
                    n = c + n0
                    wait(pe, s_xnT, n + 1)
                    wait(pe, s_qf, 2 * n)
                    wait(pe, s_kf, 4 * n - 2)
                    m.matmul(ps[:, 2, :], wt["q", a], xnT[:, h, :], start=True, stop=True)
                    if a == 2:
                        wait(pe, s_cxT, c + 1)
                    m.matmul(ps[:, 3, :], wt["k", a], src[:, h, :], start=True, stop=True).then_inc(s_qkp, 1)
                    wait(pe, s_v0, n)
                    wait(pe, s_v1, n)
                    for z in range(2):
                        o = ps[64 * z:64 * z + 64, 4, :]
                        wv = wt["v", a].rearrange("p (g h d) -> p g h d", h=2, d=HD)[:, :, z, :]
                        for k in range(2 * CP):
                            last = m.matmul(o[:, k * 64:(k + 1) * 64], src[:, h, k * S:(k + 1) * S], wv,
                                            start=True, stop=True)
                    last.then_inc(s_vp, 1)

                def relative(c, ks):
                    if isinstance(c, int) and c == 0 and ks[0] == 0:
                        pe.wait_ge(s_relw, 1)
                        pe.wait_ge(s_bo, 1)
                    wait(pe, s_qf, 2 * c + 1)
                    for k in ks:
                        t = c * CP + k
                        wait(pe, s_re0, t - 1)
                        wait(pe, s_re1, t - 1)
                        lhs = qk[:, 0, :].rearrange("p (c q) -> p q c", q=CP)[:, k, :]
                        for z in range(2):
                            last = m.matmul(ps[:, RELBANK[k % 2][z], :], lhs, relw[:, z * HP:(z + 1) * HP, :],
                                            start=True, stop=True)
                        last.then_inc(s_relp, 1)

                def project(lead, follow):
                    if follow:
                        queries_keys_values(*follow[:2])
                    if follow and a == 1:
                        relative(follow[0], (0, 1))
                    if lead:
                        transposes(*lead)
                        if a == 1 and isinstance(lead[0], int) and lead[0] == 0:
                            output_biases()
                    if follow and a == 1:
                        relative(follow[0], (2, 3))
                pipe(pe, project)
                pe.wait_ge(s_v0, n0 + NCH)
                pe.wait_ge(s_v1, n0 + NCH)
                pe.wait_ge(s_qf, 2 * (n0 + NCH))
                pe.wait_ge(s_kf, 4 * (n0 + NCH))
                if a == 1:
                    pe.wait_ge(s_re0, NPAIR)
                    pe.wait_ge(s_re1, NPAIR)

                def attend(t, u, i):
                    if live(t, u, i, 0):
                        z = u % 2
                        if u % 4 == 0:
                            pe.wait_ge(s_st[u // 4], 16 * 4 * len(RUNS) * (i + 1 + (a - 1) * NCH // 2))
                        if a == 1:
                            wait(pe, s_add, t - 1)
                        else:
                            wait(pe, s_sc, t - 1)
                        for b in range(2):
                            for h in range(HP):
                                k = (u % 4) * S
                                last = m.matmul(ps[:, 2 * z + b, h * S:(h + 1) * S],
                                                Qst[0:KROWS, u // 4, b * HP + h, :, :]
                                                .rearrange("p b (i q) -> p q (b i)", q=CP)[:, u % 4, :],
                                                Kst[0:KROWS, u // 4, b * HP + h, k:k + S],
                                                start=(h == 0), stop=(h == HP - 1),
                                                skip_group_check=True)
                        last.then_inc(s_qk, 1)
                    if live(t, u, i, 2):
                        z = u % 2
                        wait(pe, s_p, t + t0 - 1)
                        for b in range(2):
                            wait(pe, (s_e0, s_e1)[b], t + t0 - 2)
                            for k in range(4):
                                last = m.transpose(ps[:, 4 + b, k * 128:(k + 1) * 128],
                                                   P[:, z, (b * 4 + k) * 128:(b * 4 + k + 1) * 128], ident[:, :])
                            last.then_inc(s_t, 1)
                    if live(t, u, i, 3):
                        z = (u - 3) % 2
                        wait(pe, s_e0, t + t0 - 2)
                        wait(pe, s_e1, t + t0 - 2)
                        wait(pe, s_on, 2 * (t + t0 - 3))
                        for g in range(HP):
                            last = m.matmul(ps[:, 6, g * 2 * VW:(g + 1) * 2 * VW], PT[:, z, g * 128:(g + 1) * 128],
                                            V[:, bass.ds((t - 3) * 2, 2), g, :], start=True, stop=True)
                        last.then_inc(s_pv, 1)
                    if u % 4 == 3 and live(t, u, i, 7):
                        cs = ((u - 7) % 8) // 4
                        if isinstance(t, int):
                            cn = (t + t0 - 3) // 4
                        else:
                            cn = i * 2 + (u - 3) // 4 + (a - 1) * NCH
                        wait(pe, s_on, 8 * cn)
                        wait(pe, s_x, cn - 1)
                        transpose_chunk(7, on[:, cs, :, :], s_ot)
                    if u % 4 == 0 and live(t, u, i, 5):
                        if isinstance(t, int):
                            cn = t // 4 - 1 + n0
                            if t < 8:
                                return
                        else:
                            cn = i * 2 + u // 4 - 1 + n0
                        wait(pe, s_onT, cn)
                        for k in range(CP):
                            last = m.matmul(ps[:, 7, k * 128:(k + 1) * 128], onT[:, k * 128:(k + 1) * 128],
                                            wt["o", a], start=True, stop=True)
                        last.then_inc(s_wo, 1)
                steps(pe, attend, 5)

            pe.wait_ge(s_sc, NPAIR)
            pe.wait_ge(s_e1, 2 * NPAIR)
            pe.wait_ge(s_on, 4 * NPAIR)

            pe.wait_ge(s_selb, 1)

            def up(c, h, k):
                wait(pe, s_g, 4 * c + k - 1)
                m.matmul(ps[:, 4 + k % 2, :], w1[:, k * 128:(k + 1) * 128], xnT[:, h, :],
                         start=True, stop=True).then_inc(s_h, 1)

            def transposes(c, h):
                n = c + 2 * NCH
                wait(pe, s_xn, n + 1)
                wait(pe, s_xnT, n)
                transpose_chunk(0, xn, s_xtp)

            def logits(c, h):
                wait(pe, s_xnT, c + 2 * NCH + 1)
                wait(pe, s_dg, c)
                m.matmul(ps[:, 1, 0:CP * E], ones[0:1, :], bg[0:1, :].unsqueeze(1).broadcast_to([1, CP, E]),
                         start=True, stop=False, skip_group_check=True)
                for k in range(CP):
                    last = m.matmul(ps[:, 1, k * E:(k + 1) * E], xnT[:, h, k * 128:(k + 1) * 128], wg[:, :],
                                    start=False, stop=(k == CP - 1), skip_group_check=True)
                last.then_inc(s_lgp, 1)

            def spread(c):
                wait(pe, s_cf, c + 1)
                wait(pe, s_cfT, c)
                for k in range(CP):
                    last = m.transpose(ps[0:NSPLIT * E, 2, k * 64:(k + 1) * 64].bitcast(BF16),
                                       coefp[:, k, :, :].rearrange("p s e -> p (s e)"), identb[:, :])
                last.then_inc(s_cfp, 1)
                wait(pe, s_cfT, c + 1)

            def gate_rows(c, k):
                wait(pe, s_hw, 4 * c + k - 1)
                m.matmul(ps[:, 3 if k % 2 else 6, :], selb[:, k * 128:(k + 1) * 128], coefT[:, :],
                         start=True, stop=True).then_inc(s_hb, 1)

            def down(c, k):
                wait(pe, s_hw, 4 * c + k + 1)
                if k == 0:
                    if isinstance(c, int) and c == 0:
                        pe.wait_ge(s_x, 2 * NCH)
                    wait(pe, s_y, c)
                for q in range(CP):
                    last = m.matmul(ps[:, 7, q * 128:(q + 1) * 128], hw[:, k % 2, q * 128:(q + 1) * 128],
                                    w2[:, k, :], start=(k == 0 and q == 0), stop=(k == NC4 - 1),
                                    skip_group_check=True)
                last.then_inc(s_yo, 1)

            def ffn(lead, follow):
                if follow:
                    c, h = follow[:2]
                    up(c, h, 0)
                    spread(c)
                    gate_rows(c, 0)
                    up(c, h, 1)
                if lead:
                    transposes(*lead[:2])
                if follow:
                    gate_rows(c, 1)
                    up(c, h, 2)
                if lead:
                    logits(*lead[:2])
                if follow:
                    down(c, 0)
                    gate_rows(c, 2)
                    up(c, h, 3)
                    down(c, 1)
                    gate_rows(c, 3)
                    down(c, 2)
                    down(c, 3)
            pipe(pe, ffn)


def kernel(**inputs):
    import numpy as np
    import concourse.bacc as bacc
    from concourse.bass_utils import run_bass_kernel_spmd

    nc = bacc.Bacc("TRN2", target_bir_lowering=False, num_devices=1)
    arrays = {}

    def put(name, a):
        a = np.ascontiguousarray(a)
        arrays["in_" + name] = a
        return nc.dram_tensor("in_" + name, a.shape, mybir.dt.from_np(a.dtype), kind="ExternalInput").ap()

    g = {k: np.asarray(v) for k, v in inputs.items()}
    x = put("x", g["x"])
    c = put("ctx", g["ctx_1024"])
    w = {}
    def dh(m):
        return m.reshape(*m.shape[:-1], H, HD).swapaxes(-1, -2).reshape(m.shape)
    order = {"q": dh, "k": dh, "v": lambda m: m, "o": lambda m: m}
    W = np.stack([np.stack([order[n](g[f"L0_attn_W{n}"]) for n in "qkvo"], 1),
                  np.stack([order[n](g[f"L0_xattn_W{n}"].T) for n in "qkvo"], 1)])
    w["W"] = put("W", W)
    kinds = ("attn", "xattn")
    w["bcol"] = put("bcol", np.stack([np.stack([order[n](g[f"L0_{t}_b{n}"]) for n in "qkv"], 1) for t in kinds], 1))
    w["brow"] = put("brow", np.stack([g[f"L0_{t}_bo"] for t in kinds])[None])
    w["sel"] = put("sel", np.tile(np.repeat(np.eye(E, dtype=np.float32), R, axis=1), (NSPLIT, 1)))
    w["rel"] = put("rel", g["L0_attn_rel_key"][-S:].T)
    w["Wg"] = put("Wg", g["L0_ffn_Wg"].T)
    w["bg"] = put("bg", g["L0_ffn_bg"].reshape(1, E))
    w["W1"] = put("W1", g["L0_ffn_W1"].reshape(E * R, D).T)
    w["W2"] = put("W2", g["L0_ffn_W2"].transpose(0, 2, 1).reshape(E * R, D))
    out = nc.dram_tensor("out", (B, S, D), F32, kind="ExternalOutput").ap()
    build(nc, x, c, w, out)
    r = run_bass_kernel_spmd(nc, [arrays], core_ids=[0])
    return r.results[0]["out"]
```

```python
import concourse.bass as bass
import concourse.mybir as mybir
from concourse.alu_op_type import AluOpType as ALU

F32 = mybir.dt.float32
BF16 = mybir.dt.bfloat16
U32 = mybir.dt.uint32
ACT = mybir.ActivationFunctionType
AX = mybir.AxisListType

B, S, D = 64, 64, 128
H, HD = 16, 8
HP = H // 2
NPAIR = B // 2
CP = 4
NCH = NPAIR // CP
CT = CP * 128
HALF = CT // 2
SC = H * S
E, R = 8, 64
NC4 = E * R // 128
TOPK = 2
LORA = 2.0
EPS = 1e-5
NEG = -1.0e30
NSPLIT = 3
NPROD = 6
RUNS = ((0, 3, 0), (3, 2, 1), (5, 1, 2))
KROWS = 64 + NPROD * HD
VW = 18


def build(nc, x_in, ctx_in, w, out):
    from contextlib import ExitStack
    ctx = ExitStack()
    with ctx:
        def sb(name, shape, dt=F32):
            return ctx.enter_context(nc.sbuf_tensor(name, shape, dt))

        def sem(name):
            return ctx.enter_context(nc.semaphore(name))

        X = sb("X", [128, NPAIR, D])
        ident = sb("ident", [128, 128])
        identb = sb("identb", [128, 128], BF16)
        maskneg = sb("maskneg", [128, S])
        ones = sb("ones", [1, 128])
        wall = sb("wall", [128, 2, 4, D])
        wt = {(n, a): wall[:, a - 1, k, :] for a in (1, 2) for k, n in enumerate("qkvo")}
        bcol = sb("bcol", [128, 2, 3])
        brow = sb("brow", [1, 2, D])
        borep = sb("borep", [128, 2, D])
        relrep = sb("relrep", [128, S])
        headrow = sb("headrow", [128, H])
        relw = sb("relw", [128, H, S])
        wg = sb("wg", [128, E])
        bg = sb("bg", [1, E])
        w1 = sb("w1", [128, E * R])
        w2 = sb("w2", [128, NC4, D])
        selw = sb("selw", [NSPLIT * E, E * R])
        selb = sb("selb", [NSPLIT * E, E * R], BF16)
        iota8 = sb("iota8", [128, E])
        nhalf = sb("nhalf", [128, CP])
        ecst = sb("ecst", [128, CP])
        Qst = sb("Qst", [128, 2, H, 2, HALF], BF16)
        Kst = sb("Kst", [128, 2, H, HALF], BF16)
        V = sb("V", [128, NPAIR * 2, HP, VW])
        st6 = sb("st6", [128, CP, 6])
        mv = sb("mv", [128, CP, 2])
        veps = sb("veps", [128, CP])
        rstd = sb("rstd", [128, CP])
        xn = sb("xn", [128, CP, D])
        xnT = sb("xnT", [128, 2, CT])
        qk = sb("qk", [128, 2, CT])
        qkr = sb("qkr", [128, 2, CT])
        parts = sb("parts", [128, 2, 2, NSPLIT, CT], BF16)
        relst = sb("relst", [128, CP, SC + 1])
        relsh = sb("relsh", [128, 4, SC])
        cx = relst[:, 2, 0:SC].rearrange("p (s q d) -> p s q d", s=2, d=D)
        cxT = relst[:, 3, 0:SC].rearrange("p (s c) -> p s c", s=2)
        SS = relst[:, 0:2, 0:SC].rearrange("p s (h j) -> p s h j", j=S)
        negm = sb("negm", [128, 2, H])
        P = sb("P", [128, 2, SC])
        PT = sb("PT", [128, 2, SC])
        idle = sb("idle", [128, 1])
        zero = sb("zero", [128, 1])
        rden = sb("rden", [128, H])
        on = sb("on", [128, 2, CP, D])
        onT = sb("onT", [128, CT])
        lg = sb("lg", [128, CP, E])
        mx = sb("mx", [128, CP, 8])
        ix = sb("ix", [128, CP, 8], U32)
        ixf = sb("ixf", [128, CP, TOPK])
        dgate = sb("dgate", [128, CP])
        egate = sb("egate", [128, CP])
        gate = sb("gate", [128, TOPK, CP])
        eq = sb("eq", [128, TOPK, CP, E])
        coef = sb("coef", [128, CP, E])
        coefr = sb("coefr", [128, CP, E])
        coefp = sb("coefp", [128, CP, NSPLIT, E], BF16)
        coefT = sb("coefT", [NSPLIT * E, CT], BF16)
        hg = relsh[:, 0, :].rearrange("p (s c) -> p s c", s=2)
        hw = relsh[:, 1, :].rearrange("p (s c) -> p s c", s=2)
        yst = relsh[:, 2, :].rearrange("p (s q d) -> p s q d", s=2, d=D)

        partD = nc.dram_tensor("parts_scratch", [2, NCH, 2, NSPLIT, 2, HD, H, HALF], BF16, kind="Internal")
        PART = 2 * 128 * HALF
        relD = nc.dram_tensor("rel_scratch", [NPAIR, 128, SC + 1], F32, kind="Internal")

        ps = ctx.enter_context(nc.psum_tensor("ps", [128, 8, 512], F32))

        s_x0 = sem("s_x0")
        s_xr = sem("s_xr")
        s_w1 = sem("s_w1")
        s_w2 = sem("s_w2")
        s_rel = sem("s_rel")
        s_head = sem("s_head")
        s_relw = sem("s_relw")
        s_bop = sem("s_bop")
        s_bo = sem("s_bo")
        s_xb = sem("s_xb")
        s_selb = sem("s_selb")
        s_ms = sem("s_ms")
        s_sz = sem("s_sz")
        s_zo = sem("s_zo")
        s_vz = sem("s_vz")
        s_cst = sem("s_cst")
        s_ctx = [sem(f"s_ctx{h}") for h in range(2)]
        s_stat = sem("s_stat")
        s_rstd = sem("s_rstd")
        s_xn = sem("s_xn")
        s_xtp = sem("s_xtp")
        s_xnT = sem("s_xnT")
        s_ctp = sem("s_ctp")
        s_cxT = sem("s_cxT")
        s_qp = sem("s_qp")
        s_kp = sem("s_kp")
        s_qf = sem("s_qf")
        s_kf = sem("s_kf")
        s_r = sem("s_r")
        s_p2 = sem("s_p2")
        s_q3 = sem("s_q3")
        s_k3 = sem("s_k3")
        s_pw = [sem(f"s_pw{h}") for h in range(2)]
        s_vp = sem("s_vp")
        s_v0 = sem("s_v0")
        s_v1 = sem("s_v1")
        s_relp = sem("s_relp")
        s_re0 = sem("s_re0")
        s_rm = sem("s_rm")
        s_re1 = sem("s_re1")
        s_rw = [sem(f"s_rw{r}") for r in range(CP)]
        s_st = [sem(f"s_st{h}") for h in range(2)]
        s_rl = [sem(f"s_rl{h}") for h in range(4)]
        s_qk = sem("s_qk")
        s_add = sem("s_add")
        s_sc = sem("s_sc")
        s_mx = sem("s_mx")
        s_sub = sem("s_sub")
        s_p = sem("s_p")
        s_t = sem("s_t")
        s_e0 = sem("s_e0")
        s_e1 = sem("s_e1")
        s_pv = sem("s_pv")
        s_on = sem("s_on")
        s_ot = sem("s_ot")
        s_onT = sem("s_onT")
        s_wo = sem("s_wo")
        s_x = sem("s_x")
        c_dve = [sem(f"c_dve{n}") for n in range(5)]
        s_lgp = sem("s_lgp")
        s_dg = sem("s_dg")
        s_eg = sem("s_eg")
        s_cf = sem("s_cf")
        s_cfp = sem("s_cfp")
        s_cfT = sem("s_cfT")
        s_h = sem("s_h")
        s_hb = sem("s_hb")
        s_g = sem("s_g")
        s_hw = sem("s_hw")
        s_y = sem("s_y")
        s_yo = sem("s_yo")
        s_out = [sem(f"s_out{h}") for h in range(2)]

        NW1, NW2 = 16 * 3, 16 * 6

        def wait(eng, s, n):
            if isinstance(n, int) and n <= 0:
                return
            eng.wait_ge(s, n)

        def chunks(eng, body):
            for h in range(2):
                body(h, h, 0)
            with eng.Fori(1, NCH // 2) as i:
                for h in range(2):
                    body(i * 2 + h, h, i)

        def pipe(eng, body, begin=True):
            if begin:
                body(*FIRST)
            body((1, 1, 0), (0, 0, 0))
            with eng.Fori(1, NCH // 2) as i:
                body((i * 2, 0, i), (i * 2 - 1, 1, i - 1))
                body((i * 2 + 1, 1, i), (i * 2, 0, i))
            body(None, (NCH - 1, 1, NCH // 2 - 1))

        FIRST = ((0, 0, 0), None)

        def steps(eng, body, last, hooks=()):
            for u in range(8):
                body(u, u, 0)
            with eng.Fori(1, NPAIR // 8) as i:
                for u in range(8):
                    body(i * 8 + u, u, i)
            for u in range(last + 1):
                if u in hooks:
                    hooks[u]()
                if u < last:
                    body(NPAIR + u, u, None)

        def live(t, u, i, lag):
            if i is None:
                return u - lag < 0
            return not isinstance(t, int) or t >= lag

        def slot2(u):
            return u % 2

        RELBANK = ((6, 7), (1, 5))

        block = ctx.enter_context(nc.Block())

        @block.sync
        def _(sp):
            xv = x_in.rearrange("(q b) s d -> (b s) q d", b=2)
            sp.dma_start(X[:, 0:CP, :], xv[:, 0:CP, :]).then_inc(s_x0, 16)
            sp.dma_start(wall[:, 0, :, :], w["W"][0]).then_inc(s_w1, 16)
            sp.dma_start(bcol[:, :, :], w["bcol"]).then_inc(s_w1, 16)
            sp.dma_start(brow[:, :, :], w["brow"]).then_inc(s_w1, 16)
            sp.dma_start(relrep[:, :], bass.AP(w["rel"].tensor, 0, [[S, HD], [0, H], [1, S]])).then_inc(s_rel, 16)
            sp.dma_start(X[:, CP:NPAIR, :], xv[:, CP:NPAIR, :]).then_inc(s_xr, 16)
            sp.dma_start(wall[:, 1, :, :], w["W"][1]).then_inc(s_w2, 16)
            sp.dma_start(wg[:, :], w["Wg"]).then_inc(s_w2, 16)
            sp.dma_start(bg[:, :], w["bg"]).then_inc(s_w2, 16)
            sp.dma_start(w1[:, :], w["W1"]).then_inc(s_w2, 16)
            sp.dma_start(w2[:, :, :], w["W2"].rearrange("(c p) d -> p c d", p=128)).then_inc(s_w2, 16)
            sp.dma_start(selw[:, :], w["sel"]).then_inc(s_w2, 16)

            for a in (1, 2):
                n0 = (a - 1) * NCH

                def load_stack(c, h, pars=(0, 1)):
                    wait(sp, s_qk, (c - 1) * CP + (a - 1) * NPAIR)
                    base = ((a - 1) * NCH + c) * 2 * NSPLIT * PART
                    for par in pars:
                        for m0, nm, part in RUNS:
                            rows = slice(64 * par + m0 * HD, 64 * par + (m0 + nm) * HD)
                            first = base + part * PART + par * PART // 2
                            sp.dma_start(Qst[rows, h, :, par, :],
                                         bass.AP(partD, first, [[0, nm], [H * HALF, HD], [1, H * HALF]])
                                         ).then_inc(s_st[h], 16)
                            first = base + NSPLIT * PART + par * PART // 2
                            sp.dma_start(Kst[rows, h, :, :],
                                         bass.AP(partD, first, [[PART, nm], [H * HALF, HD], [1, H * HALF]])
                                         ).then_inc(s_st[h], 16)

                def load_rel(t, k):
                    wait(sp, s_add, t - 3)
                    src = bass.AP(relD, t * 128 * (SC + 1) + (S - 1), [[64 * (SC + 1), 2], [SC, 64], [1, SC]])
                    sp.dma_start(relsh[:, k, :], src).then_inc(s_rl[k], 16)

                def project(c, h):
                    wait(sp, s_q3, c + 1 + n0)
                    wait(sp, s_k3, c + 1 + n0)
                    for z in range(2):
                        sp.dma_start(
                            bass.AP(partD, (((a - 1) * NCH + c) * 2 + z) * NSPLIT * PART,
                                    [[HALF, 128], [128 * HALF, NSPLIT * 2], [1, HALF]]),
                            parts[:, h, z, :, :].rearrange("p s (b c) -> p (s b) c", b=2)).then_inc(s_pw[h], 16)
                    if a == 1:
                        for r in range(CP):
                            t = c * CP + r
                            wait(sp, s_rm, t + 1)
                            wait(sp, s_re1, t + 1)
                            sp.dma_start(bass.AP(relD, t * 128 * (SC + 1), [[SC + 1, 128], [1, SC + 1]]),
                                         relst[:, r, :]).then_inc(s_rw[r], 16)

                project(0, 0)
                with sp.Fori(1, NCH // 2 - 1) as i:
                    project(i * 2 - 1, 1)
                    project(i * 2, 0)
                if a == 1:
                    sp.wait_ge(s_sz, 2)
                    load_stack(0, 0)
                    project(NCH - 3, 1)
                    for r in range(CP):
                        load_rel(r, r)
                    load_stack(1, 1, (0,))
                    project(NCH - 2, 0)
                    load_stack(1, 1, (1,))
                    project(NCH - 1, 1)
                else:
                    load_stack(0, 0, (0,))
                    project(NCH - 3, 1)
                    load_stack(0, 0, (1,))
                    project(NCH - 2, 0)
                    load_stack(1, 1, (0,))
                    project(NCH - 1, 1)
                    load_stack(1, 1, (1,))

                for h in range(2):
                    sp.wait_ge(s_pw[h], 32 * (NCH // 2) * a)
                if a == 1:
                    for r in range(CP):
                        sp.wait_ge(s_rw[r], 16 * NCH)

                def attend(c, h):
                    if a == 1:
                        for r in range(CP):
                            load_rel((c + 1) * CP + r, r)
                    load_stack(c + 2, h)
                with sp.Fori(0, NCH // 2 - 1) as i:
                    for h in range(2):
                        attend(i * 2 + h, h)
                if a == 1:
                    for r in range(CP):
                        load_rel((NCH - 1) * CP + r, r)

            def store(c, h, i):
                wait(sp, s_y, c + 1)
                outv = out.rearrange("(q b) s d -> (b s) q d", b=2)
                sp.dma_start(outv[:, bass.ds(c * CP, CP), :], yst[:, h, :, :]).then_inc(s_out[h], 16)
            chunks(sp, store)
            for h in range(2):
                sp.wait_ge(s_out[h], 16 * (NCH // 2))

        @block.gpsimd
        def _(pool):
            g = nc.gpsimd
            g.memset(ident[:, :], 0.0).then_inc(s_ms, 1)
            g.memset(maskneg[:, :], 0.0).then_inc(s_ms, 1)
            g.memset(ones[:, :], 1.0).then_inc(s_ms, 1)
            g.memset(nhalf[:, :], -0.5).then_inc(s_ms, 1)
            g.memset(ecst[:, :], 2.718281828459045).then_inc(s_ms, 1)
            g.iota(iota8[:, :], pattern=[[1, E]], base=0, channel_multiplier=0,
                   allow_small_or_imprecise_dtypes=True).then_inc(s_ms, 1)
            pool.wait_ge(s_ms, 6)
            g.affine_select(out=ident[:, :], in_=ident[:, :], compare_op=ALU.not_equal, fill=1.0,
                            base=0, pattern=[[-1, 128]], channel_multiplier=1).then_inc(s_cst, 1)
            for par in range(2):
                pool.wait_ge(s_cst, 1 + par)
                v = maskneg[par * 64:par * 64 + 64, :]
                g.affine_select(out=v, in_=v, compare_op=ALU.is_ge, fill=NEG, base=1 - S,
                                pattern=[[1, S]], channel_multiplier=1).then_inc(s_cst, 1)
            pool.wait_ge(s_cst, 3)
            g.tensor_copy(identb[:, :], ident[:, :]).then_inc(s_cst, 1)
            g.memset(relst[:, :, SC:SC + 1], NEG).then_inc(s_cst, 1)

            def power(n):
                wait(pool, s_stat, n + 1)
                g.tensor_tensor(rstd[:, :], veps[:, :], nhalf[:, :], ALU.pow).then_inc(s_rstd, 1)

            def stages(a):
                n0 = (a - 1) * NCH
                t0 = (a - 1) * NPAIR

                def project(lead, follow):
                    if lead:
                        c, h, k = lead
                        power(c + n0)
                        if a == 1 and isinstance(c, int) and c == 0:
                            g.memset(Qst[:, :, :, :, :].rearrange("p a b c d -> p (a b c d)").bitcast(F32),
                                     0.0).then_inc(s_sz, 1)
                            g.memset(Kst[:, :, :, :].rearrange("p a b c -> p (a b c)").bitcast(F32),
                                     0.0).then_inc(s_sz, 1)
                    if follow:
                        c, h, k = follow
                        if a == 2 and not (isinstance(c, int) and c == 0):
                            third_part(c - 1, 1 - h)
                        wait(pool, s_qf, 2 * (c + n0 + 1))
                        wait(pool, s_q3, c + n0)
                        g.tensor_tensor(qkr[:, 0, :], qk[:, 0, :], parts[:, h, 0, 0, :],
                                        ALU.subtract).then_inc(s_r, 1)
                        if a == 1:
                            third_part(c, h)
                            for r in range(CP):
                                t = c * CP + r
                                wait(pool, s_re0, t + 1)
                                o = relst[:, r, 0:512].rearrange("p (h j) -> p h j", j=S)
                                g.tensor_tensor(o, o, maskneg[:, :].unsqueeze(1).broadcast_to([128, HP, S]),
                                                ALU.add).then_inc(s_rm, 1)

                def third_part(c, h):
                    if a == 2:
                        wait(pool, s_kf, 4 * (c + n0) + 4)
                        g.tensor_tensor(parts[:, h, 1, 2, :], qkr[:, 1, :], parts[:, h, 1, 1, :],
                                        ALU.subtract).then_inc(s_k3, 1)
                    wait(pool, s_p2, c + n0 + 1)
                    g.tensor_tensor(parts[:, h, 0, 2, :], qkr[:, 0, :], parts[:, h, 0, 1, :],
                                    ALU.subtract).then_inc(s_q3, 1)
                def projected():
                    if a == 2:
                        third_part(NCH - 1, 1)

                def attend(t, u, i):
                    wait(pool, s_mx, t + t0 + 1)
                    v = SS[:, slot2(u), :, :]
                    g.tensor_tensor(v, v, negm[:, slot2(u), :].unsqueeze(2).broadcast_to([128, H, S]),
                                    ALU.add).then_inc(s_sub, 1)
                    if u % 4 == 1:
                        wait(pool, s_xn, n0 + NCH)
                        if a == 1 and isinstance(t, int):
                            pool.wait_ge(s_bo, 1)
                        xs = X[:, bass.ds(t - 1, CP), :]
                        g.tensor_tensor(xs, xs, borep[:, a - 1:a, :].broadcast_to([128, CP, D]),
                                        ALU.add).then_inc(s_xb, 1)

                return project, projected, attend

            for a in (1, 2):
                project, projected, attend = stages(a)
                pipe(pool, project)
                projected()
                steps(pool, attend, 0)

            def ffn(c, h, i):
                power(c + 2 * NCH)
                wait(pool, s_dg, c + 1)
                g.tensor_tensor(egate[:, :], ecst[:, :], dgate[:, :], ALU.pow).then_inc(s_eg, 1)
            chunks(pool, ffn)

        @block.scalar
        def _(act):
            A = nc.scalar
            ctxv = ctx_in.rearrange("(q b) s d -> (b s) q d", b=2)
            def clear_v(half):
                A.copy(V[:, half * NPAIR:(half + 1) * NPAIR, :, :].rearrange("p b g w -> p (b g w)"),
                       zero[:, :].broadcast_to([128, NPAIR * HP * VW])).then_inc(s_vz, 1)

            act.wait_ge(s_zo, 1)
            clear_v(0)
            act.wait_ge(s_w1, NW1)
            def load_context(c, h):
                wait(act, s_ctp, c - 1)
                act.dma_start(cx[:, h, :, :], ctxv[:, bass.ds(c * CP, CP), :]).then_inc(s_ctx[h], 16)

            def stages(a):
                n0 = (a - 1) * NCH
                t0 = (a - 1) * NPAIR

                def project(lead, follow):
                    if lead and a == 2 and not (isinstance(lead[0], int) and lead[0] < 2):
                        load_context(lead[0], lead[1])
                    if follow:
                        c, h, k = follow
                        wait(act, s_qp, c + n0 + 1)
                        qv = ps[:, 2, :].rearrange("p (q b i) -> p b i q", b=2, i=S)
                        wait(act, s_r, c + n0)
                        if a == 1:
                            wait(act, s_relp, c * CP)
                        A.activation(qk[:, 0, :].rearrange("p (b i q) -> p b i q", b=2, i=S), qv,
                                     ACT.Identity, bias=bcol[:, a - 1, 0:1]).then_inc(s_qf, 1)
                        wait(act, s_kp, c + n0 + 1)
                        wait(act, s_kf, 4 * (c + n0))
                        A.activation(qk[:, 1, :].rearrange("p (b q i) -> p b q i", b=2, i=S),
                                     ps[:, 3, :].rearrange("p (q b i) -> p b q i", b=2, i=S),
                                     ACT.Identity, bias=bcol[:, a - 1, 1:2]).then_inc(s_kf, 1)
                        wait(act, s_pw[h], 32 * (k + n0 // 2))
                        wait(act, s_qf, 2 * (c + n0) + 1)
                        A.copy(parts[:, h, 0, 0, :], qk[:, 0, :]).then_inc(s_qf, 1)
                        if a == 1 and isinstance(c, int) and c == 0:
                            act.wait_ge(s_vz, 4)
                        wait(act, s_vp, c + n0 + 1)
                        A.copy(V[0:64, bass.ds(c * 2 * CP, 2 * CP), :, 0:HD],
                               ps[0:64, 4, :].rearrange("p (b g d) -> p b g d", g=HP, d=HD)).then_inc(s_v0, 1)
                        A.copy(V[64:128, bass.ds(c * 2 * CP, 2 * CP), :, HD:2 * HD],
                               ps[64:128, 4, :].rearrange("p (b g d) -> p b g d", g=HP, d=HD)).then_inc(s_v1, 1)

                    def second_part(c, h):
                        wait(act, s_r, c + n0 + 1)
                        A.copy(parts[:, h, 0, 1, :], qkr[:, 0, :]).then_inc(s_p2, 1)

                    def copy_relative(c, rs):
                        for r in rs:
                            t = c * CP + r
                            wait(act, s_relp, t + 1)
                            wait(act, s_rw[r], c * 16)
                            A.copy(relst[:, r, 0:512], ps[:, RELBANK[r % 2][0], :]).then_inc(s_re0, 1)

                    if follow and a == 1:
                        second_part(follow[0], follow[1])
                        copy_relative(follow[0], (0, 1))
                    if lead:
                        c, h, k = lead
                        wait(act, s_xtp, c + n0 + 1)
                        wait(act, s_vp, c + n0 - 1)
                        A.copy(xnT[:, h, :], ps[:, 0, :]).then_inc(s_xnT, 1)
                        if a == 1 and isinstance(c, int) and c == 0:
                            clear_v(1)
                        if a == 2:
                            wait(act, s_ctp, c + 1)
                            A.copy(cxT[:, h, :], ps[:, 1, :]).then_inc(s_cxT, 1)
                    if follow and a == 1:
                        copy_relative(follow[0], (2, 3))
                    if follow and a == 2:
                        second_part(follow[0], follow[1])

                def attend(t, u, i):
                    if a == 2 and live(t, u, i, 0):
                        wait(act, s_qk, t + t0 + 1)
                        wait(act, s_p, t + t0 - 1)
                        A.copy(SS[:, u % 2, :, :].rearrange("p h j -> p (h j)"),
                               ps[:, 2 * (u % 2):2 * (u % 2) + 2, :].rearrange("p k c -> p (k c)")).then_inc(s_sc, 1)
                    if live(t, u, i, 1):
                        v = (u - 1) % 2
                        wait(act, s_t, 2 * (t + t0 - 2))
                        wait(act, s_sub, t + t0)
                        A.activation(P[:, v, :], SS[:, v, :, :].rearrange("p h j -> p (h j)"), ACT.Exp,
                                     scale=HD ** -0.5 if a == 1 else 1.0).then_inc(s_p, 1)
                    if live(t, u, i, 2):
                        wait(act, s_t, 2 * (t + t0 - 2) + 1)
                        wait(act, s_pv, t + t0 - 3)
                        A.copy(PT[:, u % 2, 0:512], ps[:, 4, :]).then_inc(s_e0, 1)
                        if a == 1:
                            wait(act, s_t, 2 * (t + t0 - 1))
                            A.copy(PT[:, u % 2, 512:1024], ps[:, 5, :]).then_inc(s_e1, 1)
                    if u % 4 == 3 and live(t, u, i, 4):
                        if isinstance(t, int):
                            cn = (t + t0 - 3) // 4
                        else:
                            cn = i * 2 + (u - 3) // 4 + (a - 1) * NCH
                        wait(act, s_ot, cn)
                        A.copy(onT[:, :], ps[:, 7, :]).then_inc(s_onT, 1)
                return project, attend

            def ffn(lead, follow):
                def ranks(c, r):
                    wait(act, s_h, 4 * c + r + 1)
                    wait(act, s_hw, 4 * c + r - 1)
                    A.activation(hg[:, r % 2, :], ps[:, 4 + r % 2, :], ACT.Gelu).then_inc(s_g, 1)
                if follow:
                    c = follow[0]
                    ranks(c, 0)
                    wait(act, s_cfp, c + 1)
                    wait(act, s_hb, 4 * c)
                    A.copy(coefT[:, :], ps[0:NSPLIT * E, 2, 0:CT // 2].bitcast(BF16)).then_inc(s_cfT, 1)
                    ranks(c, 1)
                if lead:
                    c, h, k = lead
                    wait(act, s_xtp, c + 2 * NCH + 1)
                    wait(act, s_h, 4 * (c - 1))
                    A.copy(xnT[:, h, :], ps[:, 0, :]).then_inc(s_xnT, 1)
                if follow:
                    ranks(follow[0], 2)
                    ranks(follow[0], 3)

            project1, attend1 = stages(1)
            project2, attend2 = stages(2)

            def first_contexts():
                for h in range(2):
                    load_context(h, h)
            pipe(act, project1)
            steps(act, attend1, 4, {0: first_contexts, 2: lambda: project2(*FIRST)})
            act.wait_ge(s_pv, NPAIR)
            pipe(act, project2, begin=False)
            act.wait_ge(s_w2, NW2)
            A.copy(selb[:, :], selw[:, :]).then_inc(s_selb, 1)
            steps(act, attend2, 4, {2: lambda: ffn(*FIRST)})
            pipe(act, ffn, begin=False)

        @block.vector
        def _(dve):
            v = nc.vector
            v.memset(zero[:, :], 0.0).then_inc(s_zo, 1)

            class Chain:
                def __init__(self, s, per):
                    self.s, self.per, self.n, self.base = s, per, 0, 0

                def at(self, i):
                    self.base, self.n = (i * self.per if i is not None else self.base), 0 if i is not None else self.n

                def link(self, ins):
                    ins.then_inc(self.s, 1)
                    self.n += 1
                    dve.wait_ge(self.s, self.base + self.n)

            def stats(n, c, ch):
                if isinstance(n, int) and n <= 1:
                    dve.wait_ge((s_x0, s_xr)[n], 16)
                wait(dve, s_rstd, n)
                for k in range(CP):
                    last = v.bn_stats(st6[:, k, :], X[:, c * CP + k, :])
                ch.link(last)
                v.memset(idle[:, :], 0.0)
                for k in range(CP):
                    last = v.bn_aggr(mv[:, k, :], st6[:, k, :])
                ch.link(last)
                v.tensor_scalar(veps[:, :], mv[:, :, 1], EPS, None, ALU.add).then_inc(s_stat, 1)

            def norm(n, c):
                wait(dve, s_rstd, n + 1)
                wait(dve, s_xtp, n)
                for k in range(CP):
                    last = v.tensor_scalar(xn[:, k, :], X[:, c * CP + k, :], mv[:, k, 0:1], rstd[:, k:k + 1],
                                           ALU.subtract, ALU.mult)
                last.then_inc(s_xn, 1)

            def stages(a):
                n0 = (a - 1) * NCH
                t0 = (a - 1) * NPAIR
                chp = Chain(c_dve[a - 1], 2 * 2)

                def project(lead, follow):
                    if lead and not (a == 2 and follow and isinstance(lead[0], int)):
                        c, h, k = lead
                        if h == 0:
                            chp.at(k)
                        if a == 2:
                            dve.wait_ge(s_x, c + 1)
                        stats(c + n0, c, chp)
                        norm(c + n0, c)
                    if follow:
                        c, h, k = follow
                        wait(dve, s_pw[h], 32 * (k + n0 // 2))
                        dve.wait_ge(s_kf, 4 * (c + n0) + 1)
                        v.tensor_copy(parts[:, h, 1, 0, :], qk[:, 1, :]).then_inc(s_kf, 1)
                        dve.wait_ge(s_kf, 4 * (c + n0) + 2)
                        if a == 2:
                            wait(dve, s_k3, c + n0)
                        v.tensor_tensor(qkr[:, 1, :], qk[:, 1, :], parts[:, h, 1, 0, :],
                                        ALU.subtract).then_inc(s_kf, 1)
                        dve.wait_ge(s_kf, 4 * (c + n0) + 3)
                        v.tensor_copy(parts[:, h, 1, 1, :], qkr[:, 1, :]).then_inc(s_kf, 1)
                        if a == 1:
                            dve.wait_ge(s_kf, 4 * (c + n0) + 4)
                            v.tensor_tensor(parts[:, h, 1, 2, :], qkr[:, 1, :], parts[:, h, 1, 1, :],
                                            ALU.subtract).then_inc(s_k3, 1)
                    if lead:
                        c, h, k = lead
                        if a == 1 and isinstance(c, int) and c == 0:
                            dve.wait_ge(s_cst, 5)
                            v.tensor_reduce(headrow[:, :], ident[:, :].rearrange("p (d h) -> p h d", h=H), AX.X,
                                            ALU.add).then_inc(s_head, 1)
                            dve.wait_ge(s_head, 1)
                            dve.wait_ge(s_rel, 16)
                            v.tensor_tensor(relw[:, :, :], relrep[:, :].unsqueeze(1).broadcast_to([128, H, S]),
                                            headrow[:, :].unsqueeze(2).broadcast_to([128, H, S]),
                                            ALU.mult).then_inc(s_relw, 1)
                            dve.wait_ge(s_vz, 2)
                            v.memset(V[0:64, :, :, 2 * HD:2 * HD + 1], 1.0).then_inc(s_vz, 1)
                            v.memset(V[64:128, :, :, 2 * HD + 1:VW], 1.0).then_inc(s_vz, 1)
                    if follow:
                        c, h, k = follow
                        if a == 1:
                            for r in range(CP):
                                t = c * CP + r
                                wait(dve, s_relp, t + 1)
                                wait(dve, s_rw[r], c * 16)
                                v.tensor_tensor(relst[:, r, 512:1024].rearrange("p (h j) -> p h j", j=S),
                                                ps[:, RELBANK[r % 2][1], :].rearrange("p (h j) -> p h j", j=S),
                                                maskneg[:, :].unsqueeze(1).broadcast_to([128, HP, S]),
                                                ALU.add).then_inc(s_re1, 1)

                def attend(t, u, i):
                    if live(t, u, i, 0):
                        z = u % 2
                        if a == 1:
                            wait(dve, s_qk, t + 1)
                            wait(dve, s_p, t - 1)
                            dve.wait_ge(s_rl[u % 4], 16 * (i * 2 + u // 4 + 1))
                            v.tensor_tensor(SS[:, z, :, :].rearrange("p h j -> p (h j)"),
                                            ps[:, 2 * z:2 * z + 2, :].rearrange("p k c -> p (k c)"),
                                            relsh[:, u % 4, :], ALU.add).then_inc(s_add, 1)
                            wait(dve, s_add, t + 1)
                            wait(dve, s_sub, t - 1)
                        else:
                            wait(dve, s_sc, t + 1)
                            wait(dve, s_sub, t + t0 - 1)
                        v.tensor_reduce(negm[:, z, :], SS[:, z, :, :], AX.X, ALU.max, negate=True).then_inc(s_mx, 1)
                    if a == 2 and live(t, u, i, 2):
                        wait(dve, s_t, 2 * (t + t0 - 1))
                        wait(dve, s_pv, t + t0 - 3)
                        v.tensor_copy(PT[:, u % 2, 512:1024], ps[:, 5, :]).then_inc(s_e1, 1)
                    if live(t, u, i, 3):
                        wait(dve, s_pv, t + t0 - 2)
                        O = ps[:, 6, 0:HP * 2 * VW].rearrange("p (g b w) -> p g b w", b=2, w=VW)
                        v.reciprocal(rden[:, :].rearrange("p (g h) -> p g h", h=2),
                                     O[:, :, 0, 2 * HD:VW]).then_inc(c_dve[3], 1)
                        dve.wait_ge(c_dve[3], t + t0 - 2)
                        k = (u - 3) % 4
                        cs = ((u - 3) % 8) // 4
                        if k == 0 and (a == 2 or not isinstance(t, int) or t >= 11):
                            if isinstance(t, int):
                                cn = (t + t0 - 3) // 4
                            else:
                                cn = i * 2 + (u - 3) // 4 + (a - 1) * NCH
                            wait(dve, s_ot, cn - 1)
                        for par in range(2):
                            q = slice(par * 64, par * 64 + 64)
                            v.tensor_tensor(on[q, cs, k, :].rearrange("p (g h d) -> p g h d", h=2, d=HD),
                                            O[q, :, par, 0:2 * HD].rearrange("p g (h d) -> p g h d", d=HD),
                                            rden[q, :].rearrange("p (g h) -> p g h", h=2).unsqueeze(3)
                                            .broadcast_to([64, HP, 2, HD]), ALU.mult).then_inc(s_on, 1)
                    if u % 4 == 0 and live(t, u, i, 5):
                        if isinstance(t, int):
                            cl = t // 4 - 2
                        else:
                            cl = i * 2 + u // 4 - 2
                        if isinstance(cl, int) and cl < 0:
                            return
                        wait(dve, s_xb, cl + n0 + 1)
                        wait(dve, s_wo, cl + n0 + 1)
                        xs = X[:, bass.ds(cl * CP, CP), :].rearrange("p q d -> p (q d)")
                        v.tensor_tensor(xs, xs, ps[:, 7, :], ALU.add).then_inc(s_x, 1)
                return project, attend

            chf = Chain(c_dve[4], 2 * 15)

            def experts(c):
                wait(dve, s_lgp, c + 1)
                chf.link(v.tensor_copy(lg[:, :, :].rearrange("p q e -> p (q e)"), ps[:, 1, 0:CP * E]))
                v.memset(idle[:, :], 0.0)
                for k in range(CP):
                    last = v.max(mx[:, k, :], lg[:, k, :])
                chf.link(last)
                wait(dve, s_eg, c)
                v.tensor_tensor(dgate[:, :], mx[:, :, 1], mx[:, :, 0], ALU.subtract).then_inc(s_dg, 1)
                for k in range(CP):
                    last = v.max_index(ix[:, k, :], mx[:, k, :], lg[:, k, :])
                chf.link(last)

            def gates(c):
                chf.link(v.tensor_copy(ixf[:, :, :], ix[:, :, 0:TOPK]))
                io = iota8[:, :].unsqueeze(1).broadcast_to([128, CP, E])
                for r in range(TOPK):
                    last = v.tensor_tensor(eq[:, r, :, :], io, ixf[:, :, r:r + 1].broadcast_to([128, CP, E]),
                                           ALU.is_equal)
                chf.link(last)
                wait(dve, s_eg, c + 1)
                chf.link(v.tensor_scalar(gate[:, 1, :], egate[:, :], 1.0, None, ALU.add))
                chf.link(v.reciprocal(gate[:, 0, :], gate[:, 1, :]))
                chf.link(v.tensor_tensor(gate[:, 1, :], gate[:, 0, :], egate[:, :], ALU.mult))
                for r in range(TOPK):
                    last = v.tensor_tensor(eq[:, r, :, :], eq[:, r, :, :],
                                           gate[:, r, :].unsqueeze(2).broadcast_to([128, CP, E]), ALU.mult)
                chf.link(last)

            def gate_parts(c):
                wait(dve, s_cfp, c)
                chf.link(v.tensor_tensor(coef[:, :, :], eq[:, 0, :, :], eq[:, 1, :, :], ALU.add))
                chf.link(v.tensor_copy(coefp[:, :, 0, :], coef[:, :, :]))
                chf.link(v.tensor_tensor(coefr[:, :, :], coef[:, :, :], coefp[:, :, 0, :], ALU.subtract))
                chf.link(v.tensor_copy(coefp[:, :, 1, :], coefr[:, :, :]))
                v.tensor_tensor(coefp[:, :, 2, :], coefr[:, :, :], coefp[:, :, 1, :], ALU.subtract).then_inc(s_cf, 1)

            def weight(c, k):
                wait(dve, s_g, 4 * c + k + 1)
                wait(dve, s_hb, 4 * c + k + 1)
                wait(dve, s_yo, 4 * c + k - 1)
                v.tensor_tensor(hw[:, k % 2, :], ps[:, 3 if k % 2 else 6, :], hg[:, k % 2, :],
                                ALU.mult).then_inc(s_hw, 1)

            def residual(c, h, k):
                wait(dve, s_yo, 4 * c + 4)
                wait(dve, s_out[h], 16 * k)
                v.scalar_tensor_tensor(yst[:, h, :, :].rearrange("p q d -> p (q d)"), ps[:, 7, :], LORA,
                                       X[:, bass.ds(c * CP, CP), :].rearrange("p q d -> p (q d)"),
                                       ALU.mult, ALU.add).then_inc(s_y, 1)

            def ffn_stats(c, h, k):
                if h == 0:
                    chf.at(k)
                dve.wait_ge(s_x, c + NCH + 1)
                stats(c + 2 * NCH, c, chf)

            def ffn(lead, follow):
                second = lead and isinstance(lead[0], int)
                if lead and not second:
                    ffn_stats(*lead)
                if follow:
                    c, h, k = follow
                    if not (isinstance(c, int) and c == 0):
                        residual(c - 1, 1 - h, k - (1 - h))
                if lead and not second:
                    norm(lead[0] + 2 * NCH, lead[0])
                if follow:
                    weight(c, 0)
                    weight(c, 1)
                if lead:
                    experts(lead[0])
                if follow:
                    weight(c, 2)
                if lead:
                    gates(lead[0])
                if follow:
                    weight(c, 3)
                if lead:
                    gate_parts(lead[0])

            project1, attend1 = stages(1)
            project2, attend2 = stages(2)

            def first_norm():
                ffn_stats(0, 0, 0)
                norm(2 * NCH, 0)

            def first_gates():
                experts(0)
                gates(0)
                gate_parts(0)
                ffn_stats(1, 1, 0)
                norm(2 * NCH + 1, 1)
            pipe(dve, project1)
            dve.wait_ge(s_bop, 1)
            v.tensor_copy(borep[:, :, :].rearrange("p a d -> p (a d)"), ps[:, 7, 0:2 * D]).then_inc(s_bo, 1)
            for r in range(2):
                dve.wait_ge(s_rw[r], 16 * NCH)
            steps(dve, attend1, 5, {1: lambda: project2(*FIRST), 3: lambda: project2((1, 1, 0), None)})
            dve.wait_ge(s_pv, NPAIR)
            pipe(dve, project2, begin=False)
            steps(dve, attend2, 5, {1: first_norm, 3: first_gates})
            pipe(dve, ffn, begin=False)
            residual(NCH - 1, 1, NCH // 2 - 1)

        @block.tensor
        def _(pe):
            m = nc.tensor
            pe.wait_ge(s_cst, 5)

            pe.wait_ge(s_w1, NW1)

            def output_biases():
                pe.wait_ge(s_w2, NW2)
                for a in (1, 2):
                    o = ps[:, 7, (a - 1) * D:a * D]
                    m.matmul(o, bcol[:, a - 1, 2:3].broadcast_to([128, 128]), wt["o", a], start=True, stop=False)
                    last = m.matmul(o, ones[0:1, :], brow[0:1, a - 1, :], start=False, stop=True)
                last.then_inc(s_bop, 1)

            def transpose_chunk(bank, src, s_ready):
                for k in range(CP):
                    last = m.transpose(ps[:, bank, k * 128:(k + 1) * 128], src[:, k, :], ident[:, :])
                last.then_inc(s_ready, 1)

            def stages(a):
                n0 = (a - 1) * NCH
                t0 = (a - 1) * NPAIR

                src = xnT if a == 1 else cxT

                def transposes(c, h, k):
                    n = c + n0
                    wait(pe, s_xn, n + 1)
                    wait(pe, s_xnT, n)
                    transpose_chunk(0, xn, s_xtp)
                    if a == 2:
                        pe.wait_ge(s_ctx[h], 16 * (k + 1))
                        wait(pe, s_cxT, c)
                        transpose_chunk(1, cx[:, h, :, :], s_ctp)

                def queries_keys_values(c, h):
                    n = c + n0
                    wait(pe, s_xnT, n + 1)
                    wait(pe, s_qf, 2 * n)
                    wait(pe, s_kf, 4 * n - 3)
                    m.matmul(ps[:, 2, :], wt["q", a], xnT[:, h, :], start=True, stop=True).then_inc(s_qp, 1)
                    if a == 2:
                        wait(pe, s_cxT, c + 1)
                    m.matmul(ps[:, 3, :], wt["k", a], src[:, h, :], start=True, stop=True).then_inc(s_kp, 1)
                    wait(pe, s_v0, n)
                    wait(pe, s_v1, n)
                    for z in range(2):
                        o = ps[64 * z:64 * z + 64, 4, :]
                        wv = wt["v", a].rearrange("p (g h d) -> p g h d", h=2, d=HD)[:, :, z, :]
                        for k in range(2 * CP):
                            last = m.matmul(o[:, k * 64:(k + 1) * 64], src[:, h, k * S:(k + 1) * S], wv,
                                            start=True, stop=True)
                    last.then_inc(s_vp, 1)

                def relative(c, ks):
                    if isinstance(c, int) and c == 0 and ks[0] == 0:
                        pe.wait_ge(s_relw, 1)
                    wait(pe, s_qf, 2 * c + 1)
                    for k in ks:
                        t = c * CP + k
                        wait(pe, s_re0, t - 1)
                        wait(pe, s_re1, t - 1)
                        lhs = qk[:, 0, :].rearrange("p (c q) -> p q c", q=CP)[:, k, :]
                        for z in range(2):
                            last = m.matmul(ps[:, RELBANK[k % 2][z], :], lhs, relw[:, z * HP:(z + 1) * HP, :],
                                            start=True, stop=True)
                        last.then_inc(s_relp, 1)

                def project(lead, follow):
                    if follow and not (a == 2 and isinstance(follow[0], int) and follow[0] == 0):
                        queries_keys_values(*follow[:2])
                    if follow and a == 1:
                        relative(follow[0], (0, 1))
                    if lead:
                        transposes(*lead)
                    if follow and a == 1:
                        relative(follow[0], (2, 3))
                def projected():
                    pe.wait_ge(s_v0, n0 + NCH)
                    pe.wait_ge(s_v1, n0 + NCH)
                    pe.wait_ge(s_qf, 2 * (n0 + NCH))
                    pe.wait_ge(s_kf, 4 * (n0 + NCH))
                    if a == 1:
                        pe.wait_ge(s_re0, NPAIR)
                        pe.wait_ge(s_re1, NPAIR)

                def attend(t, u, i):
                    if live(t, u, i, 0):
                        z = u % 2
                        if u % 4 == 0:
                            pe.wait_ge(s_st[u // 4], 16 * 4 * len(RUNS) * (i + 1 + (a - 1) * NCH // 2))
                        if a == 1:
                            wait(pe, s_add, t - 1)
                        else:
                            wait(pe, s_sc, t - 1)
                        for b in range(2):
                            for h in range(HP):
                                k = (u % 4) * S
                                last = m.matmul(ps[:, 2 * z + b, h * S:(h + 1) * S],
                                                Qst[0:KROWS, u // 4, b * HP + h, :, :]
                                                .rearrange("p b (i q) -> p q (b i)", q=CP)[:, u % 4, :],
                                                Kst[0:KROWS, u // 4, b * HP + h, k:k + S],
                                                start=(h == 0), stop=(h == HP - 1),
                                                skip_group_check=True)
                        last.then_inc(s_qk, 1)
                    if live(t, u, i, 2):
                        z = u % 2
                        wait(pe, s_p, t + t0 - 1)
                        for b in range(2):
                            wait(pe, (s_e0, s_e1)[b], t + t0 - 2)
                            for k in range(4):
                                last = m.transpose(ps[:, 4 + b, k * 128:(k + 1) * 128],
                                                   P[:, z, (b * 4 + k) * 128:(b * 4 + k + 1) * 128], ident[:, :])
                            last.then_inc(s_t, 1)
                    if live(t, u, i, 3):
                        z = (u - 3) % 2
                        wait(pe, s_e0, t + t0 - 2)
                        wait(pe, s_e1, t + t0 - 2)
                        wait(pe, s_on, 2 * (t + t0 - 3))
                        for g in range(HP):
                            last = m.matmul(ps[:, 6, g * 2 * VW:(g + 1) * 2 * VW], PT[:, z, g * 128:(g + 1) * 128],
                                            V[:, bass.ds((t - 3) * 2, 2), g, :], start=True, stop=True)
                        last.then_inc(s_pv, 1)
                    if u % 4 == 3 and live(t, u, i, 7):
                        cs = ((u - 7) % 8) // 4
                        if isinstance(t, int):
                            cn = (t + t0 - 3) // 4
                        else:
                            cn = i * 2 + (u - 3) // 4 + (a - 1) * NCH
                        wait(pe, s_on, 8 * cn)
                        wait(pe, s_x, cn - 1)
                        transpose_chunk(7, on[:, cs, :, :], s_ot)
                    if u % 4 == 0 and live(t, u, i, 5):
                        if isinstance(t, int):
                            cn = t // 4 - 1 + n0
                            if t < 8:
                                return
                        else:
                            cn = i * 2 + u // 4 - 1 + n0
                        wait(pe, s_onT, cn)
                        for k in range(CP):
                            last = m.matmul(ps[:, 7, k * 128:(k + 1) * 128], onT[:, k * 128:(k + 1) * 128],
                                            wt["o", a], start=True, stop=True)
                        last.then_inc(s_wo, 1)
                return project, projected, attend, queries_keys_values

            def up(c, h, k):
                wait(pe, s_g, 4 * c + k - 1)
                m.matmul(ps[:, 4 + k % 2, :], w1[:, k * 128:(k + 1) * 128], xnT[:, h, :],
                         start=True, stop=True).then_inc(s_h, 1)

            def transposes(c, h):
                n = c + 2 * NCH
                wait(pe, s_xn, n + 1)
                wait(pe, s_xnT, n)
                transpose_chunk(0, xn, s_xtp)

            def logits(c, h):
                wait(pe, s_xnT, c + 2 * NCH + 1)
                wait(pe, s_dg, c)
                m.matmul(ps[:, 1, 0:CP * E], ones[0:1, :], bg[0:1, :].unsqueeze(1).broadcast_to([1, CP, E]),
                         start=True, stop=False, skip_group_check=True)
                for k in range(CP):
                    last = m.matmul(ps[:, 1, k * E:(k + 1) * E], xnT[:, h, k * 128:(k + 1) * 128], wg[:, :],
                                    start=False, stop=(k == CP - 1), skip_group_check=True)
                last.then_inc(s_lgp, 1)

            def spread(c):
                wait(pe, s_cf, c + 1)
                wait(pe, s_cfT, c)
                for k in range(CP):
                    last = m.transpose(ps[0:NSPLIT * E, 2, k * 64:(k + 1) * 64].bitcast(BF16),
                                       coefp[:, k, :, :].rearrange("p s e -> p (s e)"), identb[:, :])
                last.then_inc(s_cfp, 1)
                wait(pe, s_cfT, c + 1)

            def gate_rows(c, k):
                wait(pe, s_hw, 4 * c + k - 1)
                m.matmul(ps[:, 3 if k % 2 else 6, :], selb[:, k * 128:(k + 1) * 128], coefT[:, :],
                         start=True, stop=True).then_inc(s_hb, 1)

            def down(c, k):
                wait(pe, s_hw, 4 * c + k + 1)
                if k == 0:
                    if isinstance(c, int) and c == 0:
                        pe.wait_ge(s_x, 2 * NCH)
                    wait(pe, s_y, c)
                for q in range(CP):
                    last = m.matmul(ps[:, 7, q * 128:(q + 1) * 128], hw[:, k % 2, q * 128:(q + 1) * 128],
                                    w2[:, k, :], start=(k == 0 and q == 0), stop=(k == NC4 - 1),
                                    skip_group_check=True)
                last.then_inc(s_yo, 1)

            def ffn(lead, follow):
                if follow:
                    c, h = follow[:2]
                    if not (isinstance(c, int) and c == 0):
                        up(c, h, 0)
                        up(c, h, 1)
                    spread(c)
                    gate_rows(c, 0)
                    gate_rows(c, 1)
                    up(c, h, 2)
                if lead:
                    transposes(*lead[:2])
                if follow:
                    down(c, 0)
                if lead:
                    logits(*lead[:2])
                if follow:
                    gate_rows(c, 2)
                    up(c, h, 3)
                    down(c, 1)
                    gate_rows(c, 3)
                    down(c, 2)
                    down(c, 3)

            project1, projected1, attend1, _ = stages(1)
            project2, projected2, attend2, queries_keys_values2 = stages(2)

            def first_queries():
                pe.wait_ge(s_e0, NPAIR)
                queries_keys_values2(0, 0)

            def first_ups():
                pe.wait_ge(s_e0, 2 * NPAIR)
                pe.wait_ge(s_e1, 2 * NPAIR)
                up(0, 0, 0)
                up(0, 0, 1)

            def first_transposes():
                pe.wait_ge(s_add, NPAIR)
                project2(*FIRST)

            def first_logits():
                pe.wait_ge(s_sc, NPAIR)
                ffn(*FIRST)
            pipe(pe, project1)
            projected1()
            output_biases()
            steps(pe, attend1, 5, {2: first_transposes, 3: first_queries})
            pipe(pe, project2, begin=False)
            projected2()
            steps(pe, attend2, 5, {2: first_logits, 3: first_ups})
            pe.wait_ge(s_on, 4 * NPAIR)
            pe.wait_ge(s_selb, 1)
            pipe(pe, ffn, begin=False)


def kernel(**inputs):
    import numpy as np
    import concourse.bacc as bacc
    from concourse.bass_utils import run_bass_kernel_spmd

    nc = bacc.Bacc("TRN2", target_bir_lowering=False, num_devices=1)
    arrays = {}

    def put(name, a):
        a = np.ascontiguousarray(a)
        arrays["in_" + name] = a
        return nc.dram_tensor("in_" + name, a.shape, mybir.dt.from_np(a.dtype), kind="ExternalInput").ap()

    g = {k: np.asarray(v) for k, v in inputs.items()}
    x = put("x", g["x"])
    c = put("ctx", g["ctx_1024"])
    w = {}
    def dh(m):
        return m.reshape(*m.shape[:-1], H, HD).swapaxes(-1, -2).reshape(m.shape)
    order = {"q": dh, "k": dh, "v": lambda m: m, "o": lambda m: m}
    W = np.stack([np.stack([order[n](g[f"L0_attn_W{n}"]) for n in "qkvo"], 1),
                  np.stack([order[n](g[f"L0_xattn_W{n}"].T) for n in "qkvo"], 1)])
    w["W"] = put("W", W)
    kinds = ("attn", "xattn")
    w["bcol"] = put("bcol", np.stack([np.stack([order[n](g[f"L0_{t}_b{n}"]) for n in "qkv"], 1) for t in kinds], 1))
    w["brow"] = put("brow", np.stack([g[f"L0_{t}_bo"] for t in kinds])[None])
    w["sel"] = put("sel", np.tile(np.repeat(np.eye(E, dtype=np.float32), R, axis=1), (NSPLIT, 1)))
    w["rel"] = put("rel", g["L0_attn_rel_key"][-S:].T)
    w["Wg"] = put("Wg", g["L0_ffn_Wg"].T)
    w["bg"] = put("bg", g["L0_ffn_bg"].reshape(1, E))
    w["W1"] = put("W1", g["L0_ffn_W1"].reshape(E * R, D).T)
    w["W2"] = put("W2", g["L0_ffn_W2"].transpose(0, 2, 1).reshape(E * R, D))
    out = nc.dram_tensor("out", (B, S, D), F32, kind="ExternalOutput").ap()
    build(nc, x, c, w, out)
    r = run_bass_kernel_spmd(nc, [arrays], core_ids=[0])
    return r.results[0]["out"]
```
